# Optimizing a Trainium2 kernel written in Bass

```python
import numpy as np
import jax
import jax.numpy as jnp

def _softmax(x, axis=-1):
    return jax.nn.softmax(x, axis=axis)

def _gelu(x):
    return jax.nn.gelu(x, approximate=True)

def _silu(x):
    return jax.nn.silu(x)

def _sigmoid(x):
    return jax.nn.sigmoid(x)

def _layernorm(x, axis=-1, eps=1e-05):
    m = jnp.mean(x, axis=axis, keepdims=True)
    v = jnp.var(x, axis=axis, keepdims=True)
    return (x - m) / jnp.sqrt(v + eps)

def _scatter_add(tgt, idx, src, axis=0):
    return tgt.at[idx].add(src)

def _segment_sum(src, seg, n):
    return jax.ops.segment_sum(src, seg, n)
kernel_name = 'mk_prb_d1_jaxref_r4_4adf6a'

def setup_inputs(seed: int=0):
    np.random.seed(seed)
    _w = jnp.asarray

    def _L0_attn_setup():
        import jax, jax.numpy as jnp
        import numpy as np
        B, T, C = (4, 256, 512)
        QK_BITS = 64
        V_BITS = 64
        H = C // QK_BITS
        N_LAYER = 24
        LAYER_ID = 12
        SCHMITT = 0.001

        def _schmitt_bits(x, th):
            xt = jnp.moveaxis(x, 2, 0)

            def step(prev, xi):
                b = jnp.where(xi > th, 1.0, jnp.where(xi < -th, 0.0, prev))
                return (b, b)
            _, bits = jax.lax.scan(step, jnp.zeros(xt.shape[1:], x.dtype), xt)
            return jnp.moveaxis(bits, 0, 2)

        def _rosa_bits_ops(q, k, v, schmitt_trigger):
            qb = 2.0 * _schmitt_bits(q, schmitt_trigger) - 1.0
            kb = 2.0 * _schmitt_bits(k, schmitt_trigger) - 1.0
            vb = jax.nn.sigmoid(v)
            sim = jnp.einsum('bhtk,bhjk->bhtj', qb, kb)
            Tq = q.shape[2]
            causal = jnp.tril(jnp.ones((Tq, Tq), dtype=bool))
            attn = jax.nn.softmax(jnp.where(causal, sim, -jnp.inf), axis=-1)
            return jnp.einsum('bhtj,bhjv->bhtv', attn, vb)
        key = jax.random.key(seed)
        k_x, k_q, k_k, k_v = jax.random.split(key, 4)
        x = jax.random.normal(k_x, (B, T, C), dtype=jnp.float32)
        ratio = 1.0 - LAYER_ID / N_LAYER
        ddd = (jnp.arange(C, dtype=jnp.float32) / C).reshape(1, 1, C)
        x_q = 1.0 - ddd ** (0.9 * ratio)
        x_k = 1.0 - ddd ** (0.7 * ratio)
        x_v = 1.0 - ddd ** (0.7 * ratio)
        s = 1.0 / np.sqrt(C)
        Wq = jax.random.uniform(k_q, (H * QK_BITS, C), jnp.float32, -0.5 * s, 0.5 * s)
        Wk = jax.random.uniform(k_k, (H * QK_BITS, C), jnp.float32, -0.05 * s, 0.05 * s)
        Wv = jax.random.uniform(k_v, (C, H * V_BITS), jnp.float32, -0.5 * s, 0.5 * s)
        emb0 = jnp.full((1, 1, H * V_BITS), -1.0, dtype=jnp.float32)
        emb1 = jnp.full((1, 1, H * V_BITS), +1.0, dtype=jnp.float32)
        return {'x': x, 'x_q': x_q, 'x_k': x_k, 'x_v': x_v, 'Wq': Wq, 'Wk': Wk, 'Wv': Wv, 'emb0': emb0, 'emb1': emb1}
    _L0_attn_in = _L0_attn_setup()

    def _L0_ffn_setup():
        import jax, jax.numpy as jnp
        import numpy as np
        B, T, D, E, F, K, ND = (2, 64, 512, 64, 128, 4, 4)
        H = F * K
        N_SHARED = 2
        key = jax.random.key(seed)
        ks = jax.random.split(key, 12)
        s = lambda k, shape: jax.random.normal(k, shape, jnp.float32) * 0.02
        x = jax.random.normal(ks[0], (B, T, D), jnp.float32)
        Wr = s(ks[1], (E, D))
        router_bias = jnp.zeros((E,), jnp.float32)
        affinity = s(ks[2], (E, ND))
        te_W1 = s(ks[3], (D // 2, D))
        te_b1 = jnp.zeros((D // 2,), jnp.float32)
        te_W2 = s(ks[4], (ND, D // 2))
        te_b2 = jnp.zeros((ND,), jnp.float32)
        Wg = s(ks[5], (E, D, F))
        Wu = s(ks[6], (E, D, F))
        Wd = s(ks[7], (E, F, D))
        Sg = s(ks[8], (N_SHARED, D, H))
        Su = s(ks[9], (N_SHARED, D, H))
        Sd = s(ks[10], (N_SHARED, H, D))
        return dict(x=x, Wr=Wr, router_bias=router_bias, affinity=affinity, te_W1=te_W1, te_b1=te_b1, te_W2=te_W2, te_b2=te_b2, Wg=Wg, Wu=Wu, Wd=Wd, Sg=Sg, Su=Su, Sd=Sd)
    _L0_ffn_in = _L0_ffn_setup()
    _d = {'L0_attn_x': _L0_attn_in['x'], 'L0_attn_x_q': _L0_attn_in['x_q'], 'L0_attn_x_k': _L0_attn_in['x_k'], 'L0_attn_x_v': _L0_attn_in['x_v'], 'L0_attn_Wq': _L0_attn_in['Wq'], 'L0_attn_Wk': _L0_attn_in['Wk'], 'L0_attn_Wv': _L0_attn_in['Wv'], 'L0_attn_emb0': _L0_attn_in['emb0'], 'L0_attn_emb1': _L0_attn_in['emb1'], 'L0_ffn_Wr': _L0_ffn_in['Wr'], 'L0_ffn_router_bias': _L0_ffn_in['router_bias'], 'L0_ffn_affinity': _L0_ffn_in['affinity'], 'L0_ffn_te_W1': _L0_ffn_in['te_W1'], 'L0_ffn_te_b1': _L0_ffn_in['te_b1'], 'L0_ffn_te_W2': _L0_ffn_in['te_W2'], 'L0_ffn_te_b2': _L0_ffn_in['te_b2'], 'L0_ffn_Wg': _L0_ffn_in['Wg'], 'L0_ffn_Wu': _L0_ffn_in['Wu'], 'L0_ffn_Wd': _L0_ffn_in['Wd'], 'L0_ffn_Sg': _L0_ffn_in['Sg'], 'L0_ffn_Su': _L0_ffn_in['Su'], 'L0_ffn_Sd': _L0_ffn_in['Sd']}
    _x0 = _d['L0_attn_x']
    _d['L0_attn_x'] = jax.random.normal(jax.random.fold_in(jax.random.key(seed), 1), (1, 2048, 512), dtype=_x0.dtype)
    del _x0
    return _d

def reference(L0_attn_x, L0_attn_x_q, L0_attn_x_k, L0_attn_x_v, L0_attn_Wq, L0_attn_Wk, L0_attn_Wv, L0_attn_emb0, L0_attn_emb1, L0_ffn_Wr, L0_ffn_router_bias, L0_ffn_affinity, L0_ffn_te_W1, L0_ffn_te_b1, L0_ffn_te_W2, L0_ffn_te_b2, L0_ffn_Wg, L0_ffn_Wu, L0_ffn_Wd, L0_ffn_Sg, L0_ffn_Su, L0_ffn_Sd):

    def _L0_attn_ref(x, x_q, x_k, x_v, Wq, Wk, Wv, emb0, emb1):
        import jax, jax.numpy as jnp
        import numpy as np
        B, T, C = (4, 256, 512)
        QK_BITS = 64
        V_BITS = 64
        H = C // QK_BITS
        N_LAYER = 24
        LAYER_ID = 12
        SCHMITT = 0.001

        def _schmitt_bits(x, th):
            xt = jnp.moveaxis(x, 2, 0)

            def step(prev, xi):
                b = jnp.where(xi > th, 1.0, jnp.where(xi < -th, 0.0, prev))
                return (b, b)
            _, bits = jax.lax.scan(step, jnp.zeros(xt.shape[1:], x.dtype), xt)
            return jnp.moveaxis(bits, 0, 2)

        def _rosa_bits_ops(q, k, v, schmitt_trigger):
            qb = 2.0 * _schmitt_bits(q, schmitt_trigger) - 1.0
            kb = 2.0 * _schmitt_bits(k, schmitt_trigger) - 1.0
            vb = jax.nn.sigmoid(v)
            sim = jnp.einsum('bhtk,bhjk->bhtj', qb, kb)
            Tq = q.shape[2]
            causal = jnp.tril(jnp.ones((Tq, Tq), dtype=bool))
            attn = jax.nn.softmax(jnp.where(causal, sim, -jnp.inf), axis=-1)
            return jnp.einsum('bhtj,bhjv->bhtv', attn, vb)
        b, t, c = x.shape
        xx = jnp.concatenate([jnp.zeros((b, 1, c), x.dtype), x[:, :-1]], axis=1) - x
        xq = (x + xx * x_q) @ Wq.T
        xk = (x + xx * x_k) @ Wk.T
        xv = (x + xx * x_v) @ Wv.T
        xq = xq.reshape(b, t, H, QK_BITS).transpose(0, 2, 1, 3)
        xk = xk.reshape(b, t, H, QK_BITS).transpose(0, 2, 1, 3)
        xv = xv.reshape(b, t, H, V_BITS).transpose(0, 2, 1, 3)
        xo = _rosa_bits_ops(xq, xk, xv, SCHMITT)
        xo = xo.transpose(0, 2, 1, 3).reshape(b, t, H * V_BITS)
        return emb1 * xo + emb0 * (1.0 - xo)

    def _L0_ffn_ref(x, Wr, router_bias, affinity, te_W1, te_b1, te_W2, te_b2, Wg, Wu, Wd, Sg, Su, Sd):
        import jax, jax.numpy as jnp
        import numpy as np
        B, T, D, E, F, K, ND = (2, 64, 512, 64, 128, 4, 4)
        H = F * K
        N_SHARED = 2
        b, t, d = x.shape
        n = b * t
        flat = x.reshape(n, d)
        xm = x.mean(axis=1)
        h1 = jax.nn.gelu(xm @ te_W1.T + te_b1, approximate=False)
        task_dist = jax.nn.softmax(h1 @ te_W2.T + te_b2, axis=-1)
        dom = task_dist @ affinity.T
        logits = (flat @ Wr.T).reshape(b, t, E) + 0.5 * dom[:, None, :]
        logits = logits.reshape(n, E)
        scores = jax.nn.softmax(logits, axis=-1)
        _, topk_idx = jax.lax.top_k(logits + router_bias, K)
        topk_scores = jnp.take_along_axis(scores, topk_idx, axis=-1)
        topk_scores = topk_scores / (topk_scores.sum(-1, keepdims=True) + 1e-08)
        combine = jnp.zeros((n, E), x.dtype).at[jnp.arange(n)[:, None], topk_idx].add(topk_scores)
        g = jnp.einsum('nd,edf->enf', flat, Wg)
        u = jnp.einsum('nd,edf->enf', flat, Wu)
        h = jax.nn.silu(g) * u
        hw = h * combine.T[:, :, None]
        out = jnp.einsum('enf,efd->nd', hw, Wd)
        for i in range(Sg.shape[0]):
            sh = jax.nn.silu(flat @ Sg[i]) * (flat @ Su[i])
            out = out + sh @ Sd[i]
        return out.reshape(b, t, d)
    x = L0_attn_x
    xn = _layernorm(x, axis=-1)
    x = x + _L0_attn_ref(xn, L0_attn_x_q, L0_attn_x_k, L0_attn_x_v, L0_attn_Wq, L0_attn_Wk, L0_attn_Wv, L0_attn_emb0, L0_attn_emb1) + _L0_ffn_ref(xn, L0_ffn_Wr, L0_ffn_router_bias, L0_ffn_affinity, L0_ffn_te_W1, L0_ffn_te_b1, L0_ffn_te_W2, L0_ffn_te_b2, L0_ffn_Wg, L0_ffn_Wu, L0_ffn_Wd, L0_ffn_Sg, L0_ffn_Su, L0_ffn_Sd)
    return x

_drawn_inputs = setup_inputs


def setup_inputs(seed=0):
    import zlib

    import numpy as np

    out = dict(_drawn_inputs(seed))
    spreads = {'L0_attn_emb0': (-1.0, 0.2),
     'L0_attn_emb1': (1.0, 0.2),
     'L0_ffn_router_bias': (0.0, 0.8),
     'L0_ffn_te_b1': (0.0, 0.8),
     'L0_ffn_te_b2': (0.0, 0.8)}
    factors = {'L0_ffn_Wr': 4.643,
     'L0_ffn_affinity': 8.0,
     'L0_ffn_te_W1': 200.0,
     'L0_ffn_te_W2': 8.0,
     'L0_ffn_Wg': 4.491,
     'L0_ffn_Wu': 4.411,
     'L0_ffn_Wd': 4.392,
     'L0_attn_x_v': 3.275}
    for name, (base, spread) in spreads.items():
        noise = np.random.default_rng([zlib.crc32(name.encode()), seed]).standard_normal(out[name].shape)
        drawn = base * np.exp(spread * noise) if base else spread * noise
        out[name] = jnp.asarray(drawn.astype(out[name].dtype))
    for name, factor in factors.items():
        out[name] = (out[name] * factor).astype(out[name].dtype)
    return out
```

```python
from contextlib import ExitStack, contextmanager

import concourse.bass as bass
from concourse import mybir

ALU = mybir.AluOpType
ACT = mybir.ActivationFunctionType
AX_X = mybir.AxisListType.X
F32 = mybir.dt.float32
BF16 = mybir.dt.bfloat16
F16 = mybir.dt.float16
I32 = mybir.dt.int32
U32 = mybir.dt.uint32

P = 128
N = 2048
D = 512
DC = D // P
NT = N // P
CH = 512
NCH = N // CH
TPC = CH // P
H = 8
DH = D // H
VW = DH + 1
E = 64
K = 4
F = 128
NS = 8
SLOTS = NT * NS
SCORES_FREE, PROBS_FREE, SUMS_FREE, ROWS_FREE = 2, 4, 2, 1
WCOLS = DC * 2 * F + D
EPS = 1e-5
THRESHOLD = 0.001
ND = 4
assert (K * N + E * (P - 1)) // P <= SLOTS <= P

ROW_E0, ROW_E1, ROW_AFF, ROW_RB, ROW_B2 = 0, D, 2 * D, 2 * D + ND * E, 2 * D + ND * E + E
ROW_COLS = ROW_B2 + ND
COL_XQ, COL_XK, COL_XV, COL_B1 = 0, DC, 2 * DC, 3 * DC
COL_COLS = COL_B1 + 2


def at_least(eng, sem, value):
    if not (isinstance(value, int) and value <= 0):
        eng.wait_ge(sem, value)


class Own:

    def __init__(self, eng, sem):
        self.eng, self.sem, self.base, self.n = eng, sem, 0, 0

    def mark(self, ins):
        ins.then_inc(self.sem, 1)
        self.n += 1

    def wait(self):
        self.eng.wait_ge(self.sem, self.base + self.n)

    def step(self, ins):
        self.mark(ins)
        self.wait()

    @contextmanager
    def loop(self, trips, per_trip, first=0):
        outer = self.base + self.n
        with self.eng.Fori(first, first + trips) as i:
            self.base, self.n = outer - first * per_trip + i * per_trip, 0
            yield i
            assert self.n == per_trip, self.n
        self.base, self.n = outer + trips * per_trip, 0


def slot_steps(step, loop):
    for f in range(NS + 1):
        step(0, f, 0)
    with loop(NT - 2) as i:
        for f in range(1, NS + 1):
            step(i * NS, f, i)
    for f in range(1, NS):
        step((NT - 1) * NS, f, NT - 1)


def build(nc, x, wqkv, cols, rows, wr, te1, te2, wshared, wexperts, out):
    with ExitStack() as ctx:
        def sb(name, shape, dt=F32):
            return ctx.enter_context(nc.sbuf_tensor(name, shape, dt))

        def sem(name):
            return ctx.enter_context(nc.semaphore(name))

        xn_dram = nc.dram_tensor("xn_dram", [N, D], F32, kind="Internal").ap()
        part_dram = nc.dram_tensor("part_dram", [NT, P, D], F32, kind="Internal").ap()
        y_dram = nc.dram_tensor("y_dram", [SLOTS * P, D], F32, kind="Internal").ap()
        y_slots = y_dram.rearrange("(s p) d -> s p d", p=P)

        reg_a = sb("reg_a", [P, NS * WCOLS])
        wq_sb = reg_a[:, 0:3 * DC * D].rearrange("p (m c n) -> p m c n", m=3, c=DC)
        mix = reg_a[:, 3 * DC * D:6 * DC * D].rearrange("p (m c n) -> p m c n", m=3, c=DC)
        sw = reg_a[:, :].rearrange("p (u n) -> p u n", u=NS)
        acc = reg_a[:, 0:NT * D].rearrange("p (t d) -> p t d", t=NT)
        yrows = reg_a[:, NT * D:NT * D + K * D].rearrange("p (k d) -> p k d", k=K)

        reg_b = sb("reg_b", [P, NT * D])
        xs = reg_b[:, :].rearrange("p (t d) -> p t d", t=NT)
        lg = reg_b[:, 0:1024].rearrange("p (t e) -> p t e", t=NT)
        lb = reg_b[:, 1024:2048].rearrange("p (t e) -> p t e", t=NT)
        ex = reg_b[:, 2048:3072].rearrange("p (t e) -> p t e", t=NT)
        pos = reg_b[:, 3072:4096].rearrange("p (t e) -> p t e", t=NT)
        prod = reg_b[:, 4096:5120].rearrange("p (t e) -> p t e", t=NT)
        oh = reg_b[:, 5120:7168].bitcast(BF16).rearrange("p (k t e) -> p k t e", k=K, t=NT)
        cum = reg_b[:, 7168:8192].rearrange("p (t e) -> p t e", t=NT)
        ew = reg_b[:, 0:4 * WCOLS].rearrange("p (r n) -> p r n", r=4)
        xg = reg_b[:, 4 * WCOLS:4 * WCOLS + 4 * D].rearrange("p (r d) -> p r d", r=4)

        reg_c = sb("reg_c", [P, 4608])
        xx = reg_c[:, 0:DC * CH].rearrange("p (c n) -> p c n", c=DC)
        low = reg_c[:, 2048:2304].bitcast(BF16)
        high = reg_c[:, 2304:2560].bitcast(BF16)
        te1_sb = reg_c[:, 2560:3584].rearrange("p (c n) -> p c n", c=DC)
        wr_sb = reg_c[:, 3584:3840].rearrange("p (c n) -> p c n", c=DC)
        h1b = reg_c[:, 3840:4096].rearrange("p (j n) -> p j n", j=2)
        list_a = reg_c[:, 4096:4352].bitcast(F16).rearrange("p (r n) -> p r n", r=4)
        list_b = reg_c[:, 4352:4608].bitcast(F16).rearrange("p (r n) -> p r n", r=4)
        xgT = reg_c[:, 0:1024].rearrange("p (b c n) -> p b c n", b=2, c=DC)
        xst = reg_c[:, 1024:1536].rearrange("p (c n) -> p c n", c=DC)
        sg = reg_c[:, 1536:1792].rearrange("p (u n) -> p u n", u=2)
        hb = reg_c[:, 1792:2048].rearrange("p (u n) -> p u n", u=2)
        hT = reg_c[:, 2048:2304].rearrange("p (u n) -> p u n", u=2)
        ysb = reg_c[:, 2304:3328].rearrange("p (b n) -> p b n", b=2)
        psh = reg_c[:, 3328:3840]
        xt = reg_c[:, 3840:4352]
        pr = reg_c[:, 0:4096].rearrange("p (r j n) -> p r j n", r=4, j=2)
        xo = reg_c[:, 4096:4352].rearrange("p (t d) -> p t d", t=TPC)
        rden = reg_c[:, 4352:4356]

        XW = N + 8
        xnT_t = sb("xnT", [P, DC * XW])
        xnT = xnT_t[:, :].rearrange("p (c n) -> p c n", c=DC)
        kpad = xnT_t[:, 0:H * N // 2].bitcast(BF16).rearrange("p (h n) -> p h n", h=H)
        bits = [sb("qbits", [P, DC, N], BF16), sb("kbits", [P, DC, N], BF16)]
        vals = sb("vals", [P, NT, H * VW])
        rows_sb = sb("rows_sb", [P, ROW_COLS])
        cols_sb = sb("cols_sb", [P, COL_COLS])
        te2_sb = sb("te2_sb", [P, 2, ND])
        ident = sb("ident", [P, P])
        iota_e = sb("iota_e", [P, E])
        iota_s = sb("iota_s", [P, P], F16)
        tok_i = sb("tok_i", [P, NT])
        part_i = sb("part_i", [P, 1])
        before = sb("before", [P, P], BF16)
        ones_b = sb("ones_b", [P, P], BF16)
        stats = sb("stats", [P, NT, 6])
        mv = sb("mv", [P, NT, 2])
        mhalf = sb("mhalf", [P, TPC])
        rstd = sb("rstd", [P, NT])
        xm = sb("xm", [P, NCH, DC])
        h1 = sb("h1", [P, 2])
        td = sb("td", [P, 16])
        dom = sb("dom", [P, E])
        mx = sb("mx", [P, NT])
        zs = sb("zs", [P, NT])
        top = sb("top", [P, NT, 8])
        topi = sb("topi", [P, NT, 8], U32)
        topf = sb("topf", [P, NT, K])
        wgt = sb("wgt", [P, K, NT])
        wsum = sb("wsum", [P, NT])
        cnt = sb("cnt", [P, E])
        cnti = sb("cnti", [P, E], I32)
        incl = sb("incl", [P, E])
        ones_e = sb("ones_e", [P, E])
        eid = sb("eid", [P, 1])
        eid_row = sb("eid_row", [1, SLOTS], I32)
        slotf = sb("slotf", [P, K, NT])
        sloti = sb("sloti", [P, NT, K], U32)
        hii = sb("hii", [P, K, NT], I32)
        hif = sb("hif", [P, K, NT])
        lof = sb("lof", [P, K, NT])
        idx = sb("idx", [P, SLOTS], U32)
        idx_now = sb("idx_now", [P, 4], U32)
        psum = ctx.enter_context(nc.psum_tensor("psum", [P, 8, CH], F32))

        def gate_up(w, c):
            return w[:, c * 2 * F:(c + 1) * 2 * F]

        def down(w):
            return w[:, DC * 2 * F:WCOLS]

        x_in = [sem(f"x_in{g}") for g in range(NCH)]
        rows_in, cols_in, te_in, wr_in = sem("rows_in"), sem("cols_in"), sem("te_in"), sem("wr_in")
        w_in = [sem(f"w_in{m}") for m in range(3)]
        dve_own, act_own, pool_own = sem("dve_own"), sem("act_own"), sem("pool_own")
        consts = sem("consts")
        var_eps, rstd_ok, xn_ok, xn_out = sem("var_eps"), sem("rstd_ok"), sem("xn_ok"), sem("xn_out")
        xT_ps, xT_ok, xm_ok = sem("xT_ps"), sem("xT_ok"), sem("xm_ok")
        lg_ps, h1_ps, h1_ok, h1b_ok, z_ps, z_ok, z_exp = (sem(n) for n in (
            "lg_ps", "h1_ps", "h1_ok", "h1b_ok", "z_ps", "z_ok", "z_exp"))
        lg_shift, lg_exp, onehot_ok, rank_ps, count_ps = (sem(n) for n in (
            "lg_shift", "lg_exp", "onehot_ok", "rank_ps", "count_ps"))
        pair_ok, list_ps, eid_ok, eid_ps, idx_ok, eidrow_ok, route_read = (sem(n) for n in (
            "pair_ok", "list_ps", "eid_ok", "eid_ps", "idx_ok", "eidrow_ok", "route_read"))
        xx_ok, mixed, vmixed = sem("xx_ok"), [sem("mixed_q"), sem("mixed_k")], sem("vmixed")
        proj_ps, bits_read, v_read = sem("proj_ps"), sem("bits_read"), sem("v_read")
        sw_in = [sem(f"sw_in{f}") for f in range(NS)]
        ew_in = [sem(f"ew_in{r}") for r in range(4)]
        xg_in = [sem(f"xg_in{r}") for r in range(4)]
        gt_ps, xgT_ok, stage_ok = sem("gt_ps"), sem("xgT_ok"), sem("stage_ok")
        gu_ps, silu_ok, h_ok, hT_ps, hT_ok = ([sem(f"{n}_moe"), sem(f"{n}_shared")] for n in (
            "gu_ps", "silu_ok", "h_ok", "hT_ps", "hT_ok"))
        y_ps, y_ok, y_out = sem("y_ps"), sem("y_ok"), [sem("y_out0"), sem("y_out1")]
        sh_ps, part_ok, part_out, xt_in = sem("sh_ps"), sem("part_ok"), sem("part_out"), sem("xt_in")
        sh_read = sem("sh_read")
        kpad_ok, acc_in, rows_in_y, combined = sem("kpad_ok"), [sem(f"acc_in{c}") for c in range(NCH)], sem("rows_in_y"), sem("combined")
        s_ps, p_ok, masked, pv_ps, o_read, chunk_ok, fin_out = (sem(n) for n in (
            "s_ps", "p_ok", "masked", "pv_ps", "o_read", "chunk_ok", "fin_out"))

        block = ctx.enter_context(nc.Block())
        chunks = list(range(NCH))[::-1]
        pairs_of = {c: 2 * (c + 1) for c in chunks}
        pairs_before = {c: sum(H * pairs_of[b] for b in chunks if b > c) for c in chunks}
        heads_before = {c: H * sum(b > c for b in chunks) for c in chunks}

        @block.sync
        def _(sp):
            xv = x.rearrange("(t p) d -> p t d", p=P)
            for g in range(NCH):
                sp.dma_start(xs[:, g * TPC:(g + 1) * TPC, :], xv[:, g * TPC:(g + 1) * TPC, :]).then_inc(x_in[g], 16)
            sp.dma_start(cols_sb[:, :], cols).then_inc(cols_in, 16)
            sp.dma_start(wr_sb, wr).then_inc(wr_in, 16)
            sp.dma_start(te1_sb, te1).then_inc(te_in, 16)
            sp.dma_start(te2_sb[:, :, :], te2).then_inc(te_in, 16)
            for m in range(3):
                sp.dma_start(wq_sb[:, m], wqkv[m]).then_inc(w_in[m], 16)
            sp.dma_start(rows_sb[:, :], rows.to_broadcast([P, ROW_COLS])).then_inc(rows_in, 16)
            xnv = xn_dram.rearrange("(t p) d -> p t d", p=P)
            for g in range(NCH):
                sp.wait_ge(xn_ok, (g + 1) * TPC)
                sp.dma_start(xnv[:, g * TPC:(g + 1) * TPC, :], xs[:, g * TPC:(g + 1) * TPC, :]).then_inc(xn_out, 16)

            def load_expert(s, slot_in_ring):
                e = sp.value_load(eid_row[0:1, bass.ds(s, 1)], min_val=0, max_val=E - 1)
                sp.dma_start(ew[:, slot_in_ring, :], wexperts[bass.ds(e, 1)].rearrange("a p n -> p (a n)")).then_inc(
                    ew_in[slot_in_ring], 16)

            sp.wait_ge(eidrow_ok, 1)
            sp.wait_ge(route_read, 1)
            for s in range(4):
                load_expert(s, s)
            sp.wait_ge(proj_ps, NCH * 3 * DC)
            for f in range(NS):
                sp.dma_start(sw[:, f, :], wshared[f]).then_inc(sw_in[f], 16)
            sp.dma_start(xt, x[0:P, :]).then_inc(xt_in, 16)

            def step(base, f, i):
                s = base + f
                if f == 0:
                    return
                sp.wait_ge(y_ok, s)
                sp.dma_start(y_slots[bass.ds(s - 1, 1)].rearrange("a p d -> p (a d)"), ysb[:, (f - 1) % 2, :]).then_inc(
                    y_out[(f - 1) % 2], 16)
                if not isinstance(s, int) or s + 3 < SLOTS:
                    load_expert(s + 3, (f + 3) % 4)
                if f == NS:
                    sp.wait_ge(part_ok, i + 1)
                    sp.dma_start(part_dram[bass.ds(i, 1)].rearrange("a p d -> p (a d)"), psh).then_inc(part_out, 16)
                    sp.dma_start(xt, x[bass.ds((i + 1) * P, P), :]).then_inc(xt_in, 16)

            slot_steps(step, lambda n: sp.Fori(1, 1 + n))
            sp.wait_ge(y_ok, SLOTS)
            sp.dma_start(y_slots[SLOTS - 1], ysb[:, (SLOTS - 1) % 2, :]).then_inc(y_out[(SLOTS - 1) % 2], 16)
            sp.wait_ge(part_ok, NT)
            sp.dma_start(part_dram[NT - 1], psh).then_inc(part_out, 16)

            sp.wait_ge(part_out, 16 * NT)
            sp.wait_ge(sh_ps, SLOTS)
            for c in chunks:
                sp.dma_start(acc[:, c * TPC:(c + 1) * TPC, :],
                             part_dram[c * TPC:(c + 1) * TPC].rearrange("t p d -> p t d")).then_inc(acc_in[c], 16)
            ov = out.rearrange("(t p) d -> p t d", p=P)
            for n, c in enumerate(chunks):
                sp.wait_ge(chunk_ok, n + 1)
                sp.dma_start(ov[:, c * TPC:(c + 1) * TPC, :], acc[:, c * TPC:(c + 1) * TPC, :]).then_inc(fin_out, 16)
            sp.wait_ge(fin_out, 16 * NCH)

        @block.gpsimd
        def _(pool):
            own = Own(pool, pool_own)
            own.mark(pool.memset(ident[:, :], 0.0))
            own.mark(pool.memset(ones_b[:, :], 1.0))
            own.mark(pool.memset(before[:, :], 1.0))
            own.mark(pool.memset(mhalf[:, :], -0.5))
            own.mark(pool.memset(xnT[:, :, 0:1], 0.0))
            own.mark(pool.memset(ones_e[:, :], 1.0))
            own.mark(pool.memset(vals[:, :, :].rearrange("p t (h v) -> p (t h) v", h=H)[:, :, DH:VW], 1.0))
            own.mark(pool.iota(iota_e[:, :], [[1, E]], base=0, channel_multiplier=0, allow_small_or_imprecise_dtypes=True))
            own.mark(pool.iota(iota_s[:, :], [[1, P]], base=0, channel_multiplier=0, allow_small_or_imprecise_dtypes=True))
            own.mark(pool.iota(tok_i[:, :], [[P, NT]], base=0, channel_multiplier=1, allow_small_or_imprecise_dtypes=True))
            own.step(pool.iota(part_i[:, :], [[0, 1]], base=0, channel_multiplier=1, allow_small_or_imprecise_dtypes=True))
            own.step(pool.affine_select(out=ident[:, :], in_=ident[:, :], compare_op=ALU.not_equal, fill=1.0, base=0,
                                        pattern=[[-1, P]], channel_multiplier=1))
            pool.affine_select(out=before[:, :], in_=before[:, :], compare_op=ALU.is_gt, fill=0.0, base=0,
                               pattern=[[1, P]], channel_multiplier=-1).then_inc(consts, 1)

            for g in range(NCH):
                pool.wait_ge(var_eps, g + 1)
                t = slice(g * TPC, (g + 1) * TPC)
                pool.tensor_tensor(rstd[:, t], mv[:, t, 1], mhalf[:, :], ALU.pow).then_inc(rstd_ok, 1)

            pool.wait_ge(cols_in, 16)
            for c in range(NCH):
                pool.wait_ge(xT_ok, (c + 1) * TPC)
                if c:
                    pool.wait_ge(mixed[1], c)
                pool.tensor_tensor(xx, xnT[:, :, c * CH:c * CH + CH], xnT[:, :, c * CH + 1:c * CH + CH + 1],
                                   ALU.subtract).then_inc(xx_ok, 1)
                pool.wait_ge(xx_ok, c + 1)
                at_least(pool, proj_ps, c * 3 * DC)
                for d in range(DC):
                    own.mark(pool.tensor_scalar(mix[:, 2, d], xx[:, d], cols_sb[:, COL_XV + d:COL_XV + d + 1], None, ALU.mult))
                own.wait()
                pool.tensor_tensor(mix[:, 2], mix[:, 2], xnT[:, :, c * CH + 1:c * CH + CH + 1],
                                   ALU.add).then_inc(vmixed, 1)
                pool.wait_ge(vmixed, c + 1)

            def gather(s, r):
                own.step(pool.tensor_copy(idx_now[:, r:r + 1], idx[:, bass.ds(s, 1)]))
                pool.nop(nofuse=True)
                pool.indirect_dma_start(out=xg[:, r, :], out_offset=None, in_=xn_dram,
                                        in_offset=bass.IndirectOffsetOnAxis(ap=idx_now[:, r:r + 1], axis=0)).then_inc(
                    xg_in[r], 16)

            pool.wait_ge(xn_out, 16 * NCH)
            pool.wait_ge(idx_ok, 1)
            pool.wait_ge(route_read, 1)
            for s in range(4):
                gather(s, s)

            def step(base, f, i):
                s = base + f
                if f and (not isinstance(s, int) or s + 3 < SLOTS):
                    pool.wait_ge(gt_ps, s)
                    gather(s + 3, (f + 3) % 4)

            slot_steps(step, lambda n: own.loop(n, NS, 1))

            pool.wait_ge(y_out[0], 16 * SLOTS // 2)
            pool.wait_ge(y_out[1], 16 * SLOTS // 2)
            pool.wait_ge(sh_ps, SLOTS)
            for n, c in enumerate(chunks):
                with own.loop(H // 2, 1) as m:
                    pool.wait_ge(combined, m + (n * TPC + ROWS_FREE))
                    own.step(pool.tensor_copy(idx_now[:, :], sloti[:, bass.ds(m + c * TPC, 1), :].rearrange("p t k -> p (t k)")))
                    pool.nop(nofuse=True)
                    for k in range(K):
                        pool.indirect_dma_start(
                            out=yrows[:, k, :], out_offset=None, in_=y_dram,
                            in_offset=bass.IndirectOffsetOnAxis(ap=idx_now[:, k:k + 1], axis=0)).then_inc(rows_in_y, 16)
                    for hh in range(2):
                        for q in (0, 1):
                            unit = pairs_before[c] + m * (2 * pairs_of[c]) + (hh * pairs_of[c] + 2 * c + q)
                            pool.wait_ge(p_ok, unit + (1 + SCORES_FREE))
                            pool.nop(nofuse=True)
                            b = pr[:, (hh * pairs_of[c] + 2 * c + q) % 4]
                            for j in range(2):
                                o = (2 * q + j) * P
                                mk = pool.affine_select(out=b[:, j, o:o + P], in_=b[:, j, o:o + P], compare_op=ALU.is_ge,
                                                        fill=0.0, base=0, pattern=[[1, P]], channel_multiplier=-1)
                            mk.then_inc(masked, 1)

        @block.scalar
        def _(act):
            own = Own(act, act_own)
            for t in range(NT):
                act.wait_ge(xT_ps, t + 1)
                act.activation(xnT[:, :, 1 + t * P:1 + (t + 1) * P], psum[:, t % 2, :].rearrange("p (c n) -> p c n", c=DC),
                               ACT.Copy).then_inc(xT_ok, 1)
            act.wait_ge(h1_ps, 1)
            act.wait_ge(cols_in, 16)
            for j in range(2):
                g = act.activation(h1[:, j:j + 1], psum[:, 6, j:j + 1], ACT.Gelu, bias=cols_sb[:, COL_B1 + j:COL_B1 + j + 1],
                                   scale=1.0 / N)
            g.then_inc(h1_ok, 1)

            def values(c):
                for t in range(TPC):
                    u = c * 3 * DC + 2 * DC + t
                    act.wait_ge(proj_ps, u + 1)
                    act.activation(vals[:, c * TPC + t, :].rearrange("p (h v) -> p h v", h=H)[:, :, 0:DH],
                                   psum[:, u % 4, :].rearrange("p (h v) -> p h v", h=H), ACT.Sigmoid).then_inc(v_read, 1)

            values(0)
            act.wait_ge(z_ok, 1)
            act.activation(td[:, 4:8], td[:, 0:4], ACT.Exp, bias=td[:, 8:9], accum_out=td[:, 9:10]).then_inc(z_exp, 1)
            act.wait_ge(lg_shift, 1)
            act.activation(ex, ex, ACT.Exp).then_inc(lg_exp, 1)
            for c in range(1, NCH):
                values(c)

            def tokens(s, f):
                act.wait_ge(gt_ps, s + 1)
                at_least(act, gu_ps[0], s - 1)
                act.activation(xgT[:, f % 2], psum[:, 0, :].rearrange("p (c n) -> p c n", c=DC), ACT.Copy).then_inc(xgT_ok, 1)

            def stage(i):
                act.activation(xst, xnT[:, :, bass.ds(i * P + 1, P)], ACT.Copy).then_inc(stage_ok, 1)

            def silu(kind, s):
                act.wait_ge(gu_ps[kind], s + 1)
                at_least(act, h_ok[kind], s)
                act.activation(sg[:, kind], psum[:, 1 + kind, 0:F], ACT.Silu).then_inc(silu_ok[kind], 1)

            def rows_out(y, f):
                act.wait_ge(y_ps, y + 1)
                at_least(act, y_out[f % 2], 16 * (y // 2) if isinstance(y, int) else (y - f % 2) * 8)
                act.activation(ysb[:, f % 2], psum[:, 5 + f % 2, :], ACT.Copy).then_inc(y_ok, 1)

            stage(0)
            tokens(0, 0)

            def step(base, f, i):
                s = base + f
                silu(0, s)
                if f:
                    rows_out(s - 1, f - 1)
                if not isinstance(s, int) or s + 1 < SLOTS:
                    tokens(s + 1, f + 1)
                silu(1, s)
                if f == NS - 1 and not (isinstance(i, int) and i == NT - 1):
                    stage(i + 1)

            slot_steps(step, lambda n: act.Fori(1, 1 + n))
            rows_out(SLOTS - 1, SLOTS - 1)

            act.wait_ge(y_out[0], 16 * SLOTS // 2)
            act.wait_ge(y_out[1], 16 * SLOTS // 2)
            act.wait_ge(part_out, 16 * NT)
            act.nop(nofuse=True).then_inc(p_ok, SCORES_FREE)
            for c in chunks:
                with act.Fori(0, H // 2) as m:
                    for hh in range(2):
                        for p in range(pairs_of[c]):
                            n = hh * pairs_of[c] + p
                            unit = pairs_before[c] + m * (2 * pairs_of[c]) + n
                            o = CH // 2 if p == pairs_of[c] - 1 else 0
                            act.wait_ge(s_ps, unit + 1)
                            act.wait_ge(pv_ps, unit + 1)
                            act.activation(pr[:, n % 4, :, o:CH], psum[:, 2 * (n % 2):2 * (n % 2) + 2, o:CH], ACT.Exp,
                                           scale=4.0).then_inc(p_ok, 1)

        @block.tensor
        def _(pe):
            pe.wait_ge(consts, 1)
            for t in range(NT):
                pe.wait_ge(xn_ok, t + 1)
                at_least(pe, xT_ok, t - 1)
                for d in range(DC):
                    mm = pe.transpose(psum[:, t % 2, d * P:(d + 1) * P], xs[:, t, d * P:(d + 1) * P], ident[:, :])
                mm.then_inc(xT_ps, 1)
            pe.wait_ge(wr_in, 16)
            pe.wait_ge(xT_ok, NT)
            for t in range(NT):
                for d in range(DC):
                    mm = pe.matmul(psum[:, 4 + t // 8, (t % 8) * E:(t % 8 + 1) * E], xnT[:, d, 1 + t * P:1 + (t + 1) * P],
                                   wr_sb[:, d, :], start=d == 0, stop=d == DC - 1)
            mm.then_inc(lg_ps, 1)
            pe.wait_ge(te_in, 32)
            pe.wait_ge(xm_ok, 1)
            for j in range(2):
                for d in range(DC):
                    mm = pe.matmul(psum[:, 6, j:j + 1], te1_sb[:, d, j * P:(j + 1) * P], xm[:, 0, d:d + 1],
                                   start=d == 0, stop=d == DC - 1)
            mm.then_inc(h1_ps, 1)

            def project(c):
                for m in range(3):
                    pe.wait_ge(w_in[m], 16)
                    pe.wait_ge(vmixed if m == 2 else mixed[m], c + 1)
                    for n in range(DC):
                        u = c * 3 * DC + m * DC + n
                        if u >= 4:
                            v = u - 4
                            vc, vr = v // (3 * DC), v % (3 * DC)
                            if vr < 2 * DC:
                                pe.wait_ge(bits_read, vc * 2 * DC + vr + 1)
                            else:
                                pe.wait_ge(v_read, vc * TPC + vr - 2 * DC + 1)
                        for d in range(DC):
                            if m < 2:
                                mm = pe.matmul(psum[:, u % 4, :], wq_sb[:, m, d, n * P:(n + 1) * P], mix[:, m, d, :],
                                               start=d == 0, stop=d == DC - 1)
                            else:
                                mm = pe.matmul(psum[:, u % 4, :], mix[:, 2, d, n * P:(n + 1) * P], wq_sb[:, 2, d, :],
                                               start=d == 0, stop=d == DC - 1)
                        mm.then_inc(proj_ps, 1)

            project(0)
            pe.wait_ge(h1b_ok, 1)
            for j in range(2):
                mm = pe.matmul(psum[:, 7, 0:ND], h1b[:, j, :], te2_sb[:, j, :], start=j == 0, stop=j == 1)
            mm.then_inc(z_ps, 1)
            project(1)
            pe.wait_ge(onehot_ok, 1)
            for m, w in ((0, before), (1, ones_b)):
                for b in range(2):
                    for k in range(K):
                        mm = pe.matmul(psum[:, 4 + 2 * m + b, :], w[:, :], oh[:, k, b * 8:(b + 1) * 8, :].rearrange("p t e -> p (t e)"),
                                       start=k == 0, stop=k == K - 1)
                mm.then_inc(count_ps if m else rank_ps, 1)
            project(2)
            for n in range(K * NT):
                pe.wait_ge(pair_ok, n + 1)
                mm = pe.matmul(psum[:, 4, 0:P], list_a[:, n % 4, :], list_b[:, n % 4, :], start=n == 0, stop=n == K * NT - 1)
                mm.then_inc(list_ps, 1)
            pe.wait_ge(eid_ok, 1)
            pe.matmul(psum[0:1, 6, 0:P], eid[:, :], ident[:, :], start=True, stop=True).then_inc(eid_ps, 1)
            project(3)

            def transpose_tokens(s, f):
                pe.wait_ge(xg_in[f % 4], 16 * (s // 4 + 1) if isinstance(s, int) else (s - f % 4) * 4 + 16)
                at_least(pe, xgT_ok, s)
                for d in range(DC):
                    mm = pe.transpose(psum[:, 0, d * P:(d + 1) * P], xg[:, f % 4, d * P:(d + 1) * P], ident[:, :])
                mm.then_inc(gt_ps, 1)

            def up(kind, s, lhs, w):
                at_least(pe, h_ok[kind], s)
                for d in range(DC):
                    mm = pe.matmul(psum[:, 1 + kind, 0:2 * F], lhs[:, d, :], gate_up(w, d), start=d == 0, stop=d == DC - 1)
                mm.then_inc(gu_ps[kind], 1)

            def transpose_hidden(kind, s):
                pe.wait_ge(h_ok[kind], s + 1)
                at_least(pe, hT_ok[kind], s)
                pe.transpose(psum[:, 3 + kind, 0:P], hb[:, kind, :], ident[:, :]).then_inc(hT_ps[kind], 1)

            def down_expert(y, f):
                pe.wait_ge(hT_ok[0], y + 1)
                at_least(pe, y_ok, y - 1)
                pe.matmul(psum[:, 5 + f % 2, :], hT[:, 0, :], down(ew[:, f % 4]), start=True, stop=True).then_inc(y_ps, 1)

            def down_shared(y, f, tile):
                pe.wait_ge(hT_ok[1], y + 1)
                u = f % NS
                if u == 0:
                    at_least(pe, sh_read, tile)
                pe.matmul(psum[:, 7, :], hT[:, 1, :], down(sw[:, u]), start=u == 0, stop=u == NS - 1).then_inc(sh_ps, 1)

            pe.wait_ge(idx_ok, 1)
            pe.wait_ge(eidrow_ok, 1)
            pe.wait_ge(bits_read, NCH * 2 * DC)
            pe.wait_ge(v_read, NT)
            transpose_tokens(0, 0)

            def step(base, f, i):
                s = base + f
                pe.wait_ge(xgT_ok, s + 1)
                pe.wait_ge(ew_in[f % 4], 16 * (s // 4 + 1) if isinstance(s, int) else (s - f % 4) * 4 + 16)
                up(0, s, xgT[:, f % 2], ew[:, f % 4])
                if f:
                    down_expert(s - 1, f - 1)
                    transpose_hidden(1, s - 1)
                if not isinstance(s, int) or s + 1 < SLOTS:
                    transpose_tokens(s + 1, f + 1)
                u = f % NS
                tile = i if f < NS else i + 1
                if u == 0:
                    pe.wait_ge(stage_ok, tile + 1)
                pe.wait_ge(sw_in[u], 16)
                up(1, s, xst, sw[:, u])
                if f:
                    down_shared(s - 1, f - 1, i)
                transpose_hidden(0, s)

            slot_steps(step, lambda n: pe.Fori(1, 1 + n))
            down_expert(SLOTS - 1, SLOTS - 1)
            transpose_hidden(1, SLOTS - 1)
            down_shared(SLOTS - 1, SLOTS - 1, NT - 1)

            pe.wait_ge(xgT_ok, SLOTS)
            pe.nop(nofuse=True).then_inc(pv_ps, PROBS_FREE)
            for c in chunks:
                with pe.Fori(0, H // 2) as m:
                    np_ = pairs_of[c]

                    def at(n):
                        return pairs_before[c] + m * (2 * np_) + n

                    def scores(n):
                        hh, p = n // np_, n % np_
                        o = CH // 2 if p == np_ - 1 else 0
                        pe.wait_ge(p_ok, at(n) + 1)
                        for j in range(2):
                            mm = pe.matmul(psum[:, 2 * (n % 2) + j, o:CH],
                                           kpad[:, :, (2 * p + j) * P:(2 * p + j + 1) * P][:, bass.ds(m * 2 + hh, 1), :].rearrange("p a n -> p (a n)"),
                                           bits[0][:, :, c * CH + o:(c + 1) * CH][:, bass.ds(m, 1), :].rearrange("p a n -> p (a n)"),
                                           start=True, stop=True)
                        mm.then_inc(s_ps, 1)

                    def weighted(n):
                        hh, p = n // np_, n % np_
                        pe.wait_ge(p_ok, at(n) + (1 + SCORES_FREE))
                        if p >= np_ - 2:
                            pe.wait_ge(masked, 2 * heads_before[c] + m * 4 + (hh * 2 + p - (np_ - 2) + 1))
                        if p == 0:
                            pe.wait_ge(o_read, heads_before[c] + m * 2 + (hh + 1))
                        for j in range(2):
                            r = 2 * p + j - TPC * c
                            for t in range(max(r, 0), TPC):
                                mm = pe.matmul(psum[:, 4 + hh, t * VW:(t + 1) * VW], pr[:, n % 4, j, t * P:(t + 1) * P],
                                               vals[:, 2 * p + j, bass.ds(m * (2 * VW) + hh * VW, VW)],
                                               start=2 * p + j == 0 and t == 0, stop=r == t, skip_group_check=True)
                        mm.then_inc(pv_ps, 1)

                    for h in range(2):
                        pe.wait_ge(kpad_ok, m * 2 + (h + 1)) if c == chunks[0] else None
                    scores(0)
                    for n in range(2 * np_):
                        if n + 1 < 2 * np_:
                            scores(n + 1)
                        weighted(n)

        @block.vector
        def _(dve):
            own = Own(dve, dve_own)

            for g in range(NCH):
                dve.wait_ge(x_in[g], 16)
                for t in range(g * TPC, (g + 1) * TPC):
                    own.mark(dve.bn_stats(stats[:, t, :], xs[:, t, :]))
                own.wait()
                for t in range(g * TPC, (g + 1) * TPC):
                    own.mark(dve.bn_aggr(mv[:, t, :], stats[:, t, :]))
                own.wait()
                v = mv[:, g * TPC:(g + 1) * TPC, 1]
                dve.tensor_scalar(v, v, EPS, None, ALU.add).then_inc(var_eps, 1)
                if g:
                    normalise(dve, g - 1, rstd_ok, xn_ok, xs, mv, rstd)
            normalise(dve, NCH - 1, rstd_ok, xn_ok, xs, mv, rstd)
            for g in range(NCH):
                dve.wait_ge(xT_ok, (g + 1) * TPC)
                own.mark(dve.tensor_reduce(xm[:, g, :], xnT[:, :, 1 + g * CH:1 + (g + 1) * CH], AX_X, ALU.add))
            own.wait()
            own.step(dve.tensor_tensor(xm[:, 0:2, :], xm[:, 0:2, :], xm[:, 2:4, :], ALU.add))
            dve.tensor_tensor(xm[:, 0, :], xm[:, 0, :], xm[:, 1, :], ALU.add).then_inc(xm_ok, 1)

            def shift_mix(m, c):
                dve.wait_ge(xx_ok, c + 1)
                if c:
                    dve.wait_ge(proj_ps, (c - 1) * 3 * DC + (m + 1) * DC)
                for d in range(DC):
                    ins = dve.scalar_tensor_tensor(mix[:, m, d], xx[:, d], cols_sb[:, m * DC + d:m * DC + d + 1],
                                                   xnT[:, d, c * CH + 1:(c + 1) * CH + 1], ALU.mult, ALU.add)
                ins.then_inc(mixed[m], 1)

            def trigger(m, c):
                for n in range(DC):
                    u = c * 3 * DC + m * DC + n
                    dve.wait_ge(proj_ps, u + 1)
                    own.mark(dve.tensor_scalar(low, psum[:, u % 4, :], THRESHOLD, 0.5, ALU.is_gt, ALU.subtract))
                    dve.tensor_scalar(high, psum[:, u % 4, :], -THRESHOLD, 0.5, ALU.is_ge, ALU.subtract).then_inc(bits_read, 1)
                    dve.wait_ge(bits_read, c * 2 * DC + m * DC + n + 1)
                    own.wait()
                    own.step(dve.tensor_tensor_scan(bits[m][:, n, c * CH:(c + 1) * CH], high, low,
                                                    bits[m][:, n, c * CH - 1:c * CH] if c else -0.5, ALU.min, ALU.max))

            dve.wait_ge(cols_in, 16)
            shift_mix(0, 0)
            shift_mix(1, 0)
            dve.wait_ge(h1_ok, 1)
            for j in range(2):
                ins = dve.tensor_copy(h1b[:, j, :], h1[:, j:j + 1].to_broadcast([P, P]))
            ins.then_inc(h1b_ok, 1)
            for m in range(2):
                trigger(m, 0)
                shift_mix(m, 1)

            dve.wait_ge(z_ps, 1)
            dve.wait_ge(rows_in, 16)
            own.step(dve.tensor_tensor(td[:, 0:4], psum[:, 7, 0:ND], rows_sb[:, ROW_B2:ROW_B2 + ND], ALU.add))
            own.step(dve.tensor_reduce(td[:, 10:11], td[:, 0:4], AX_X, ALU.max))
            dve.tensor_scalar(td[:, 8:9], td[:, 10:11], -1.0, None, ALU.mult).then_inc(z_ok, 1)
            dve.wait_ge(z_exp, 1)
            own.step(dve.reciprocal(td[:, 11:12], td[:, 9:10]))
            own.step(dve.tensor_scalar(td[:, 12:16], td[:, 4:8], td[:, 11:12], 0.5, ALU.mult, ALU.mult))
            aff = rows_sb[:, ROW_AFF:ROW_AFF + ND * E].rearrange("p (n e) -> p n e", n=ND)
            own.step(dve.tensor_scalar(dom[:, :], aff[:, 0], td[:, 12:13], None, ALU.mult))
            for n in range(1, ND):
                own.step(dve.scalar_tensor_tensor(dom[:, :], aff[:, n], td[:, 12 + n:13 + n], dom[:, :], ALU.mult, ALU.add))
            dve.wait_ge(lg_ps, 1)
            dve.wait_ge(xn_out, 16 * NCH)
            dve.wait_ge(xT_ps, NT)
            own.step(dve.tensor_tensor(lg, psum[:, 4:6, :].rearrange("p b (t e) -> p (b t) e", e=E),
                                       dom[:, :].unsqueeze(1).to_broadcast([P, NT, E]), ALU.add))
            own.mark(dve.tensor_tensor(lb, lg, rows_sb[:, ROW_RB:ROW_RB + E].unsqueeze(1).to_broadcast([P, NT, E]), ALU.add))
            own.step(dve.tensor_reduce(mx[:, :], lg, AX_X, ALU.max))
            dve.tensor_tensor(ex, lg, mx[:, :].unsqueeze(2).to_broadcast([P, NT, E]), ALU.subtract).then_inc(lg_shift, 1)
            for t in range(NT):
                own.mark(dve.max(top[:, t, :], lb[:, t, :]))
            own.wait()
            for t in range(NT):
                own.mark(dve.max_index(topi[:, t, :], top[:, t, :], lb[:, t, :]))
            own.wait()
            own.step(dve.tensor_copy(topf[:, :, :], topi[:, :, 0:K]))
            for k in range(K):
                ins = dve.tensor_tensor(oh[:, k], iota_e[:, :].unsqueeze(1).to_broadcast([P, NT, E]),
                                        topf[:, :, k:k + 1].to_broadcast([P, NT, E]), ALU.is_equal)
            ins.then_inc(onehot_ok, 1)
            for m in range(2):
                trigger(m, 1)
                shift_mix(m, 2)

            dve.wait_ge(onehot_ok, 1)
            dve.wait_ge(lg_exp, 1)
            own.step(dve.tensor_reduce(zs[:, :], ex, AX_X, ALU.add))
            own.step(dve.reciprocal(zs[:, :], zs[:, :]))
            for k in range(K):
                own.step(dve.tensor_tensor(prod, oh[:, k], ex, ALU.mult))
                own.step(dve.tensor_reduce(wgt[:, k, :], prod, AX_X, ALU.add))
            own.step(dve.tensor_tensor(wgt[:, :, :], wgt[:, :, :], zs[:, :].unsqueeze(1).to_broadcast([P, K, NT]), ALU.mult))
            own.step(dve.tensor_reduce(wsum[:, :], wgt[:, :, :].rearrange("p k t -> p t k"), AX_X, ALU.add))
            own.step(dve.tensor_scalar(wsum[:, :], wsum[:, :], 1e-8, None, ALU.add))
            own.step(dve.reciprocal(wsum[:, :], wsum[:, :]))
            own.step(dve.tensor_tensor(wgt[:, :, :], wgt[:, :, :], wsum[:, :].unsqueeze(1).to_broadcast([P, K, NT]), ALU.mult))
            dve.wait_ge(count_ps, 1)
            counts = psum[:, 6:8, :].rearrange("p b (t e) -> p (b t) e", e=E)
            own.step(dve.tensor_scalar(cum[:, 0, :], counts[:, 0, :], 0.0, None, ALU.mult))
            for t in range(NT - 1):
                own.step(dve.tensor_tensor(cum[:, t + 1, :], counts[:, t, :], cum[:, t, :], ALU.add))
            own.step(dve.tensor_tensor(cnt[:, :], counts[:, NT - 1, :], cum[:, NT - 1, :], ALU.add))
            own.step(dve.tensor_scalar(cnti[:, :], cnt[:, :], float(P - 1), None, ALU.add))
            own.step(dve.tensor_scalar(cnti[:, :], cnti[:, :], 7, None, ALU.arith_shift_right))
            own.step(dve.tensor_copy(cnt[:, :], cnti[:, :]))
            own.step(dve.tensor_tensor_scan(incl[:, :], ones_e[:, :], cnt[:, :], 0.0, ALU.mult, ALU.add))
            own.step(dve.tensor_tensor(cnt[:, :], incl[:, :], cnt[:, :], ALU.subtract))
            own.step(dve.tensor_scalar(cnt[:, :], cnt[:, :], float(P), None, ALU.mult))
            own.step(dve.tensor_scalar(dom[:, :], incl[:, :], part_i[:, :], None, ALU.is_le, ALU.add, accum_out=eid[:, :]))
            dve.tensor_scalar(eid[:, :], eid[:, :], float(E - 1), None, ALU.min).then_inc(eid_ok, 1)
            dve.wait_ge(rank_ps, 1)
            own.step(dve.tensor_tensor(pos, psum[:, 4:6, :].rearrange("p b (t e) -> p (b t) e", e=E), cum, ALU.add))
            own.step(dve.tensor_tensor(pos, pos, cnt[:, :].unsqueeze(1).to_broadcast([P, NT, E]), ALU.add))
            for k in range(K):
                own.step(dve.tensor_tensor(prod, oh[:, k], pos, ALU.mult))
                own.step(dve.tensor_reduce(slotf[:, k, :], prod, AX_X, ALU.add))
            own.mark(dve.tensor_copy(hii[:, :, :], slotf[:, :, :]))
            dve.tensor_copy(sloti[:, :, :], slotf[:, :, :].rearrange("p k t -> p t k")).then_inc(route_read, 1)
            own.wait()
            own.step(dve.tensor_scalar(hii[:, :, :], hii[:, :, :], 7, None, ALU.arith_shift_right))
            own.step(dve.tensor_copy(hif[:, :, :], hii[:, :, :]))
            own.step(dve.scalar_tensor_tensor(lof[:, :, :], hif[:, :, :], -float(P), slotf[:, :, :], ALU.mult, ALU.add))

            def pair(n):
                t, k = n // K, n % K
                at_least(dve, list_ps, n - 3)
                dve.tensor_scalar(list_a[:, n % 4, :], iota_s[:, :], lof[:, k, t:t + 1], None, ALU.is_equal)
                dve.tensor_scalar(list_b[:, n % 4, :], iota_s[:, :], hif[:, k, t:t + 1], tok_i[:, t:t + 1],
                                  ALU.is_equal, ALU.mult).then_inc(pair_ok, 1)

            for m in range(2):
                trigger(m, 2)
                shift_mix(m, 3)
            for n in range(K * NT):
                pair(n)
            dve.wait_ge(list_ps, K * NT)
            dve.tensor_copy(idx[:, :], psum[:, 4, 0:P]).then_inc(idx_ok, 1)
            dve.wait_ge(eid_ps, 1)
            dve.tensor_copy(eid_row[:, :], psum[0:1, 6, 0:P]).then_inc(eidrow_ok, 1)
            for m in range(2):
                trigger(m, 3)

            def hidden(kind, s):
                dve.wait_ge(silu_ok[kind], s + 1)
                at_least(dve, hT_ps[kind], s)
                dve.tensor_tensor(hb[:, kind], psum[:, 1 + kind, F:2 * F], sg[:, kind], ALU.mult).then_inc(h_ok[kind], 1)

            def hidden_T(kind, s):
                dve.wait_ge(hT_ps[kind], s + 1)
                at_least(dve, y_ps if kind == 0 else sh_ps, s)
                dve.tensor_copy(hT[:, kind], psum[:, 3 + kind, 0:P]).then_inc(hT_ok[kind], 1)

            def shared_out(i):
                dve.wait_ge(sh_ps, (i + 1) * NS)
                dve.wait_ge(xt_in, 16 * (i + 1))
                at_least(dve, part_out, 16 * i)
                dve.tensor_tensor(psh, psum[:, 7, :], xt, ALU.add).then_inc(sh_read, 1)
                dve.wait_ge(sh_read, i + 1)
                dve.tensor_tensor(psh, psh, rows_sb[:, ROW_E0:ROW_E0 + D], ALU.add).then_inc(part_ok, 1)

            def step(base, f, i):
                s = base + f
                hidden(0, s)
                if f:
                    hidden_T(1, s - 1)
                hidden(1, s)
                if f == NS:
                    shared_out(i)
                hidden_T(0, s)

            slot_steps(step, lambda n: dve.Fori(1, 1 + n))
            hidden_T(1, SLOTS - 1)
            shared_out(NT - 1)

            dve.wait_ge(gu_ps[1], SLOTS)
            dve.wait_ge(stage_ok, NT)
            for h in range(H):
                own_rows, others = slice(DH * (h % 2), DH * (h % 2) + DH), slice(DH - DH * (h % 2), 2 * DH - DH * (h % 2))
                dve.memset(kpad[others, h, :].bitcast(U32), 0)
                dve.tensor_copy(kpad[own_rows, h, :], bits[1][own_rows, h // 2, :]).then_inc(kpad_ok, 1)
            own.step(dve.tensor_tensor(rows_sb[:, ROW_E1:ROW_E1 + D], rows_sb[:, ROW_E1:ROW_E1 + D],
                                       rows_sb[:, ROW_E0:ROW_E0 + D], ALU.subtract))
            dve.nop(nofuse=True).then_inc(o_read, SUMS_FREE)
            dve.nop(nofuse=True).then_inc(combined, ROWS_FREE)
            for n, c in enumerate(chunks):
                dve.wait_ge(acc_in[c], 16)
                with own.loop(H // 2, 2 * 3 + 3) as m:
                    for hh in range(2):
                        dve.wait_ge(pv_ps, m * (2 * pairs_of[c]) + (PROBS_FREE + pairs_before[c] + (hh + 1) * pairs_of[c]))
                        o = psum[:, 4 + hh, 0:TPC * VW].rearrange("p (t v) -> p t v", v=VW)
                        own.step(dve.reciprocal(rden, o[:, :, DH]))
                        dve.tensor_tensor(xo, o[:, :, 0:DH], rden.unsqueeze(2).to_broadcast([P, TPC, DH]),
                                          ALU.mult).then_inc(o_read, 1)
                        dve.wait_ge(o_read, m * 2 + (heads_before[c] + hh + 1 + SUMS_FREE))
                        own.step(dve.tensor_tensor(
                            xo, xo, rows_sb[:, bass.ds(m * (2 * DH) + (ROW_E1 + hh * DH), DH)].unsqueeze(1).to_broadcast([P, TPC, DH]),
                            ALU.mult))
                        dst = acc[:, c * TPC:(c + 1) * TPC, bass.ds(m * (2 * DH) + hh * DH, DH)]
                        own.step(dve.tensor_tensor(dst, dst, xo, ALU.add))
                    dve.wait_ge(rows_in_y, 16 * K * (n * TPC + m + 1))
                    dst = acc[:, bass.ds(m + c * TPC, 1), :].rearrange("p a d -> p (a d)")
                    for k in range(K):
                        w = wgt[:, k, bass.ds(m + c * TPC, 1)]
                        ins = dve.scalar_tensor_tensor(dst, yrows[:, k, :], w, dst, ALU.mult, ALU.add)
                        if k < K - 1:
                            own.step(ins)
                        else:
                            ins.then_inc(combined, 1)
                            dve.wait_ge(combined, m + (n * TPC + 1 + ROWS_FREE))
                dve.drain().then_inc(chunk_ok, 1)


def normalise(dve, g, rstd_ok, xn_ok, xs, mv, rstd):
    dve.wait_ge(rstd_ok, g + 1)
    for t in range(g * TPC, (g + 1) * TPC):
        dve.tensor_scalar(xs[:, t, :], xs[:, t, :], mv[:, t, 0:1], rstd[:, t:t + 1], ALU.subtract, ALU.mult).then_inc(xn_ok, 1)


def kernel(**inputs):
    import numpy as np
    import concourse.bacc as bacc
    from concourse.bass_utils import run_bass_kernel_spmd

    def get(name):
        return np.asarray(inputs[name])

    def rows_to_partitions(w):
        return w.reshape(DC, P, w.shape[1]).transpose(1, 0, 2)

    def unit_weights(gate, up, down):
        u = gate.shape[0]
        gu = np.stack([gate.reshape(u, DC, P, F), up.reshape(u, DC, P, F)], axis=3)
        gu = gu.transpose(0, 2, 1, 3, 4).reshape(u, P, DC * 2 * F)
        return np.concatenate([gu, down], axis=2)

    def split_shared(w):
        return w.reshape(2, D, NS // 2, F).transpose(0, 2, 1, 3).reshape(NS, D, F)

    def by_partition(v):
        return v.reshape(-1, P).T

    arrays = {
        "x": get("L0_attn_x").reshape(N, D),
        "wqkv": np.stack([rows_to_partitions(get(n).T) for n in ("L0_attn_Wq", "L0_attn_Wk", "L0_attn_Wv")]),
        "cols": np.concatenate([by_partition(get(n)) for n in ("L0_attn_x_q", "L0_attn_x_k", "L0_attn_x_v", "L0_ffn_te_b1")], axis=1),
        "rows": np.concatenate([get("L0_attn_emb0").reshape(-1), get("L0_attn_emb1").reshape(-1), get("L0_ffn_affinity").T.reshape(-1),
                                get("L0_ffn_router_bias"), get("L0_ffn_te_b2")]).reshape(1, ROW_COLS),
        "wr": rows_to_partitions(get("L0_ffn_Wr").T),
        "te1": rows_to_partitions(get("L0_ffn_te_W1").T),
        "te2": get("L0_ffn_te_W2").T.reshape(2, P, ND).transpose(1, 0, 2),
        "wshared": unit_weights(split_shared(get("L0_ffn_Sg")), split_shared(get("L0_ffn_Su")), get("L0_ffn_Sd").reshape(NS, F, D)),
        "wexperts": unit_weights(get("L0_ffn_Wg"), get("L0_ffn_Wu"), get("L0_ffn_Wd")),
    }
    arrays = {n: np.ascontiguousarray(a) for n, a in arrays.items()}
    nc = bacc.Bacc("TRN2", target_bir_lowering=False, num_devices=1)
    aps = [nc.dram_tensor(n, a.shape, mybir.dt.from_np(a.dtype), kind="ExternalInput").ap() for n, a in arrays.items()]
    aps.append(nc.dram_tensor("out", (N, D), F32, kind="ExternalOutput").ap())
    build(nc, *aps)
    r = run_bass_kernel_spmd(nc, [arrays], core_ids=[0])
    return r.results[0]["out"].reshape(1, N, D)
```

```python
from contextlib import ExitStack, contextmanager

import concourse.bass as bass
from concourse import mybir

ALU = mybir.AluOpType
ACT = mybir.ActivationFunctionType
AX_X = mybir.AxisListType.X
F32 = mybir.dt.float32
BF16 = mybir.dt.bfloat16
F16 = mybir.dt.float16
I32 = mybir.dt.int32
U32 = mybir.dt.uint32

P = 128
N = 2048
D = 512
DC = D // P
NT = N // P
CH = 512
NCH = N // CH
TPC = CH // P
H = 8
DH = D // H
VW = DH + 1
E = 64
K = 4
F = 128
NS = 8
SLOTS = NT * NS
SCORES_FREE, PROBS_FREE, SUMS_FREE, ROWS_FREE = 2, 4, 2, 2
WCOLS = DC * 2 * F + D
EPS = 1e-5
THRESHOLD = 0.001
ND = 4
assert (K * N + E * (P - 1)) // P <= SLOTS <= P

ROW_E0, ROW_E1, ROW_AFF, ROW_RB, ROW_B2 = 0, D, 2 * D, 2 * D + ND * E, 2 * D + ND * E + E
ROW_COLS = ROW_B2 + ND
COL_XQ, COL_XK, COL_XV, COL_B1 = 0, DC, 2 * DC, 3 * DC
COL_COLS = COL_B1 + 2


def at_least(eng, sem, value):
    if not (isinstance(value, int) and value <= 0):
        eng.wait_ge(sem, value)


class Own:

    def __init__(self, eng, sem):
        self.eng, self.sem, self.base, self.n = eng, sem, 0, 0

    def mark(self, ins):
        ins.then_inc(self.sem, 1)
        self.n += 1

    def wait(self):
        self.eng.wait_ge(self.sem, self.base + self.n)

    def step(self, ins):
        self.mark(ins)
        self.wait()

    @contextmanager
    def loop(self, trips, per_trip, first=0):
        outer = self.base + self.n
        with self.eng.Fori(first, first + trips) as i:
            self.base, self.n = outer - first * per_trip + i * per_trip, 0
            yield i
            assert self.n == per_trip, self.n
        self.base, self.n = outer + trips * per_trip, 0


def slot_steps(step, loop):
    for f in range(NS + 1):
        step(0, f, 0)
    with loop(NT - 2) as i:
        for f in range(1, NS + 1):
            step(i * NS, f, i)
    for f in range(1, NS):
        step((NT - 1) * NS, f, NT - 1)


def build(nc, x, wqkv, cols, rows, wr, te1, te2, wshared, wexperts, out):
    with ExitStack() as ctx:
        def sb(name, shape, dt=F32):
            return ctx.enter_context(nc.sbuf_tensor(name, shape, dt))

        def sem(name):
            return ctx.enter_context(nc.semaphore(name))

        xn_dram = nc.dram_tensor("xn_dram", [N, D], F32, kind="Internal").ap()
        part_dram = nc.dram_tensor("part_dram", [NT, P, D], F32, kind="Internal").ap()
        y_dram = nc.dram_tensor("y_dram", [SLOTS * P, D], F32, kind="Internal").ap()
        y_slots = y_dram.rearrange("(s p) d -> s p d", p=P)

        reg_a = sb("reg_a", [P, NS * WCOLS])
        wq_sb = reg_a[:, 0:3 * DC * D].rearrange("p (m c n) -> p m c n", m=3, c=DC)
        mix = reg_a[:, 3 * DC * D:6 * DC * D].rearrange("p (m c n) -> p m c n", m=3, c=DC)
        sw = reg_a[:, :].rearrange("p (u n) -> p u n", u=NS)
        acc = reg_a[:, 0:NT * D].rearrange("p (t d) -> p t d", t=NT)
        yrows = reg_a[:, NT * D:NT * D + 2 * K * D].rearrange("p (b k d) -> p b k d", b=2, k=K)

        reg_b = sb("reg_b", [P, NT * D])
        xs = reg_b[:, :].rearrange("p (t d) -> p t d", t=NT)
        lg = reg_b[:, 0:1024].rearrange("p (t e) -> p t e", t=NT)
        lb = reg_b[:, 1024:2048].rearrange("p (t e) -> p t e", t=NT)
        ex = reg_b[:, 2048:3072].rearrange("p (t e) -> p t e", t=NT)
        pos = reg_b[:, 3072:4096].rearrange("p (t e) -> p t e", t=NT)
        prod = reg_b[:, 4096:5120].rearrange("p (t e) -> p t e", t=NT)
        oh = reg_b[:, 5120:7168].bitcast(BF16).rearrange("p (k t e) -> p k t e", k=K, t=NT)
        cum = reg_b[:, 7168:8192].rearrange("p (t e) -> p t e", t=NT)
        ew = reg_b[:, 0:4 * WCOLS].rearrange("p (r n) -> p r n", r=4)
        xg = reg_b[:, 4 * WCOLS:4 * WCOLS + 4 * D].rearrange("p (r d) -> p r d", r=4)

        reg_c = sb("reg_c", [P, 4608])
        xx = reg_c[:, 0:DC * CH].rearrange("p (c n) -> p c n", c=DC)
        low = reg_c[:, 2048:2304].bitcast(BF16)
        high = reg_c[:, 2304:2560].bitcast(BF16)
        te1_sb = reg_c[:, 2560:3584].rearrange("p (c n) -> p c n", c=DC)
        wr_sb = reg_c[:, 3584:3840].rearrange("p (c n) -> p c n", c=DC)
        h1b = reg_c[:, 3840:4096].rearrange("p (j n) -> p j n", j=2)
        list_a = reg_c[:, 4096:4352].bitcast(F16).rearrange("p (r n) -> p r n", r=4)
        list_b = reg_c[:, 4352:4608].bitcast(F16).rearrange("p (r n) -> p r n", r=4)
        xgT = reg_c[:, 0:1024].rearrange("p (b c n) -> p b c n", b=2, c=DC)
        xst = reg_c[:, 1024:1536].rearrange("p (c n) -> p c n", c=DC)
        sg = reg_c[:, 1536:1792].rearrange("p (u n) -> p u n", u=2)
        hb = reg_c[:, 1792:2048].rearrange("p (u n) -> p u n", u=2)
        hT = reg_c[:, 2048:2304].rearrange("p (u n) -> p u n", u=2)
        ysb = reg_c[:, 2304:3328].rearrange("p (b n) -> p b n", b=2)
        psh = reg_c[:, 3328:3840]
        xt = reg_c[:, 3840:4352]
        pr = reg_c[:, 0:4096].rearrange("p (r j n) -> p r j n", r=4, j=2)
        xo = reg_c[:, 4096:4352].rearrange("p (t d) -> p t d", t=TPC)
        rden = reg_c[:, 4352:4356]

        XW = N + 8
        xnT_t = sb("xnT", [P, DC * XW])
        xnT = xnT_t[:, :].rearrange("p (c n) -> p c n", c=DC)
        keys = xnT_t[:, 0:N].bitcast(BF16).rearrange("p (h n) -> p h n", h=2)
        vst = xnT_t[:, N:N + 2 * NT * VW].rearrange("p (h t v) -> p h t v", h=2, t=NT)
        osb = xnT_t[0:VW, N + 2 * NT * VW:N + 2 * NT * VW + CH]
        bits = [sb("qbits", [P, DC, N], BF16), sb("kbits", [P, DC, N], BF16)]
        vals = sb("vals", [P, NT, H * VW])
        rows_sb = sb("rows_sb", [P, ROW_COLS])
        cols_sb = sb("cols_sb", [P, COL_COLS])
        te2_sb = sb("te2_sb", [P, 2, ND])
        ident = sb("ident", [P, P])
        iota_e = sb("iota_e", [P, E])
        iota_s = sb("iota_s", [P, P], F16)
        tok_i = sb("tok_i", [P, NT])
        part_i = sb("part_i", [P, 1])
        before = sb("before", [P, P], BF16)
        ones_b = sb("ones_b", [P, P], BF16)
        stats = sb("stats", [P, NT, 6])
        mv = sb("mv", [P, NT, 2])
        mhalf = sb("mhalf", [P, TPC])
        rstd = sb("rstd", [P, NT])
        xm = sb("xm", [P, NCH, DC])
        h1 = sb("h1", [P, 2])
        td = sb("td", [P, 16])
        dom = sb("dom", [P, E])
        mx = sb("mx", [P, NT])
        zs = sb("zs", [P, NT])
        top = sb("top", [P, NT, 8])
        topi = sb("topi", [P, NT, 8], U32)
        topf = sb("topf", [P, NT, K])
        wgt = sb("wgt", [P, K, NT])
        wsum = sb("wsum", [P, NT])
        cnt = sb("cnt", [P, E])
        cnti = sb("cnti", [P, E], I32)
        incl = sb("incl", [P, E])
        ones_e = sb("ones_e", [P, E])
        eid = sb("eid", [P, 1])
        eid_row = sb("eid_row", [1, SLOTS], I32)
        slotf = sb("slotf", [P, K, NT])
        sloti = sb("sloti", [P, NT, K], U32)
        hii = sb("hii", [P, K, NT], I32)
        hif = sb("hif", [P, K, NT])
        lof = sb("lof", [P, K, NT])
        idx = sb("idx", [P, SLOTS], U32)
        idx_now = sb("idx_now", [P, 2 * K], U32)
        psum = ctx.enter_context(nc.psum_tensor("psum", [P, 8, CH], F32))

        def gate_up(w, c):
            return w[:, c * 2 * F:(c + 1) * 2 * F]

        def down(w):
            return w[:, DC * 2 * F:WCOLS]

        x_in = [sem(f"x_in{g}") for g in range(NCH)]
        rows_in, cols_in, te_in, wr_in = sem("rows_in"), sem("cols_in"), sem("te_in"), sem("wr_in")
        w_in = [sem(f"w_in{m}") for m in range(3)]
        dve_own, act_own, pool_own = sem("dve_own"), sem("act_own"), sem("pool_own")
        consts = sem("consts")
        var_eps, rstd_ok, xn_ok, xn_out = sem("var_eps"), sem("rstd_ok"), sem("xn_ok"), sem("xn_out")
        xT_ps, xT_ok, xm_ok = sem("xT_ps"), sem("xT_ok"), sem("xm_ok")
        lg_ps, h1_ps, h1_ok, h1b_ok, z_ps, z_ok, z_exp = (sem(n) for n in (
            "lg_ps", "h1_ps", "h1_ok", "h1b_ok", "z_ps", "z_ok", "z_exp"))
        lg_shift, lg_exp, onehot_ok, rank_ps, count_ps = (sem(n) for n in (
            "lg_shift", "lg_exp", "onehot_ok", "rank_ps", "count_ps"))
        pair_ok, list_ps, eid_ok, eid_ps, idx_ok, eidrow_ok, route_read = (sem(n) for n in (
            "pair_ok", "list_ps", "eid_ok", "eid_ps", "idx_ok", "eidrow_ok", "route_read"))
        xx_ok, mixed, vmixed = sem("xx_ok"), [sem("mixed_q"), sem("mixed_k")], sem("vmixed")
        proj_ps, bits_read, v_read = sem("proj_ps"), sem("bits_read"), sem("v_read")
        sw_in = [sem(f"sw_in{f}") for f in range(NS)]
        ew_in = [sem(f"ew_in{r}") for r in range(4)]
        xg_in = [sem(f"xg_in{r}") for r in range(4)]
        gt_ps, xgT_ok, stage_ok = sem("gt_ps"), sem("xgT_ok"), sem("stage_ok")
        gu_ps, silu_ok, h_ok, hT_ps, hT_ok = ([sem(f"{n}_moe"), sem(f"{n}_shared")] for n in (
            "gu_ps", "silu_ok", "h_ok", "hT_ps", "hT_ok"))
        y_ps, y_ok, y_out = sem("y_ps"), sem("y_ok"), [sem("y_out0"), sem("y_out1")]
        sh_ps, part_ok, part_out, xt_in = sem("sh_ps"), sem("part_ok"), sem("part_out"), sem("xt_in")
        sh_read = sem("sh_read")
        staged, acc_in, combined = sem("staged"), [sem(f"acc_in{c}") for c in range(NCH)], sem("combined")
        yrows_in = [sem("yrows_in0"), sem("yrows_in1")]
        s_ps, p_ok, masked, pv_ps, oT_ok, o_ps, o_read, unit_ok, fin_out = (sem(n) for n in (
            "s_ps", "p_ok", "masked", "pv_ps", "oT_ok", "o_ps", "o_read", "unit_ok", "fin_out"))

        block = ctx.enter_context(nc.Block())
        chunks = list(range(NCH))[::-1]
        units = [(hh, c) for hh in range(2) for c in chunks]
        pairs = [(v, p) for v, (_, c) in enumerate(units) for p in range(2 * (c + 1))]
        NU, NP = len(units), len(pairs)
        first_pair = [min(n for n, (w, _) in enumerate(pairs) if w == v) for v in range(NU)]

        def last_of(v):
            return first_pair[v] + 2 * (units[v][1] + 1)

        def first_column(c, p):
            return CH // 2 if p == 2 * c + 1 else 0

        @block.sync
        def _(sp):
            xv = x.rearrange("(t p) d -> p t d", p=P)
            for g in range(NCH):
                sp.dma_start(xs[:, g * TPC:(g + 1) * TPC, :], xv[:, g * TPC:(g + 1) * TPC, :]).then_inc(x_in[g], 16)
            sp.dma_start(cols_sb[:, :], cols).then_inc(cols_in, 16)
            sp.dma_start(wr_sb, wr).then_inc(wr_in, 16)
            sp.dma_start(te1_sb, te1).then_inc(te_in, 16)
            sp.dma_start(te2_sb[:, :, :], te2).then_inc(te_in, 16)
            for m in range(3):
                sp.dma_start(wq_sb[:, m], wqkv[m]).then_inc(w_in[m], 16)
            sp.dma_start(rows_sb[:, :], rows.to_broadcast([P, ROW_COLS])).then_inc(rows_in, 16)
            xnv = xn_dram.rearrange("(t p) d -> p t d", p=P)
            for g in range(NCH):
                sp.wait_ge(xn_ok, (g + 1) * TPC)
                sp.dma_start(xnv[:, g * TPC:(g + 1) * TPC, :], xs[:, g * TPC:(g + 1) * TPC, :]).then_inc(xn_out, 16)

            def load_expert(s, slot_in_ring):
                e = sp.value_load(eid_row[0:1, bass.ds(s, 1)], min_val=0, max_val=E - 1)
                sp.dma_start(ew[:, slot_in_ring, :], wexperts[bass.ds(e, 1)].rearrange("a p n -> p (a n)")).then_inc(
                    ew_in[slot_in_ring], 16)

            sp.wait_ge(eidrow_ok, 1)
            sp.wait_ge(route_read, 1)
            for s in range(4):
                load_expert(s, s)
            sp.wait_ge(proj_ps, NCH * 3 * DC)
            for f in range(NS):
                sp.dma_start(sw[:, f, :], wshared[f]).then_inc(sw_in[f], 16)
            sp.dma_start(xt, x[0:P, :]).then_inc(xt_in, 16)

            def step(base, f, i):
                s = base + f
                if f == 0:
                    return
                sp.wait_ge(y_ok, s)
                sp.dma_start(y_slots[bass.ds(s - 1, 1)].rearrange("a p d -> p (a d)"), ysb[:, (f - 1) % 2, :]).then_inc(
                    y_out[(f - 1) % 2], 16)
                if not isinstance(s, int) or s + 3 < SLOTS:
                    load_expert(s + 3, (f + 3) % 4)
                if f == NS:
                    sp.wait_ge(part_ok, i + 1)
                    sp.dma_start(part_dram[bass.ds(i, 1)].rearrange("a p d -> p (a d)"), psh).then_inc(part_out, 16)
                    sp.dma_start(xt, x[bass.ds((i + 1) * P, P), :]).then_inc(xt_in, 16)

            slot_steps(step, lambda n: sp.Fori(1, 1 + n))
            sp.wait_ge(y_ok, SLOTS)
            sp.dma_start(y_slots[SLOTS - 1], ysb[:, (SLOTS - 1) % 2, :]).then_inc(y_out[(SLOTS - 1) % 2], 16)
            sp.wait_ge(part_ok, NT)
            sp.dma_start(part_dram[NT - 1], psh).then_inc(part_out, 16)

            sp.wait_ge(part_out, 16 * NT)
            sp.wait_ge(sh_ps, SLOTS)
            for c in chunks:
                sp.dma_start(acc[:, c * TPC:(c + 1) * TPC, :],
                             part_dram[c * TPC:(c + 1) * TPC].rearrange("t p d -> p t d")).then_inc(acc_in[c], 16)
            ov = out.rearrange("(t p) d -> p t d", p=P)
            for n, c in enumerate(chunks):
                sp.wait_ge(unit_ok, (H // 2) * NU - NCH + n + 1)
                sp.dma_start(ov[:, c * TPC:(c + 1) * TPC, :], acc[:, c * TPC:(c + 1) * TPC, :]).then_inc(fin_out, 16)
            sp.wait_ge(fin_out, 16 * NCH)

        @block.gpsimd
        def _(pool):
            own = Own(pool, pool_own)
            own.mark(pool.memset(ident[:, :], 0.0))
            own.mark(pool.memset(ones_b[:, :], 1.0))
            own.mark(pool.memset(before[:, :], 1.0))
            own.mark(pool.memset(mhalf[:, :], -0.5))
            own.mark(pool.memset(xnT[:, :, 0:1], 0.0))
            own.mark(pool.memset(ones_e[:, :], 1.0))
            own.mark(pool.memset(vals[:, :, :].rearrange("p t (h v) -> p (t h) v", h=H)[:, :, DH:VW], 1.0))
            own.mark(pool.iota(iota_e[:, :], [[1, E]], base=0, channel_multiplier=0, allow_small_or_imprecise_dtypes=True))
            own.mark(pool.iota(iota_s[:, :], [[1, P]], base=0, channel_multiplier=0, allow_small_or_imprecise_dtypes=True))
            own.mark(pool.iota(tok_i[:, :], [[P, NT]], base=0, channel_multiplier=1, allow_small_or_imprecise_dtypes=True))
            own.step(pool.iota(part_i[:, :], [[0, 1]], base=0, channel_multiplier=1, allow_small_or_imprecise_dtypes=True))
            own.step(pool.affine_select(out=ident[:, :], in_=ident[:, :], compare_op=ALU.not_equal, fill=1.0, base=0,
                                        pattern=[[-1, P]], channel_multiplier=1))
            pool.affine_select(out=before[:, :], in_=before[:, :], compare_op=ALU.is_gt, fill=0.0, base=0,
                               pattern=[[1, P]], channel_multiplier=-1).then_inc(consts, 1)

            for g in range(NCH):
                pool.wait_ge(var_eps, g + 1)
                t = slice(g * TPC, (g + 1) * TPC)
                pool.tensor_tensor(rstd[:, t], mv[:, t, 1], mhalf[:, :], ALU.pow).then_inc(rstd_ok, 1)

            pool.wait_ge(cols_in, 16)
            for c in range(NCH):
                pool.wait_ge(xT_ok, (c + 1) * TPC)
                if c:
                    pool.wait_ge(mixed[1], c)
                pool.tensor_tensor(xx, xnT[:, :, c * CH:c * CH + CH], xnT[:, :, c * CH + 1:c * CH + CH + 1],
                                   ALU.subtract).then_inc(xx_ok, 1)
                pool.wait_ge(xx_ok, c + 1)
                at_least(pool, proj_ps, c * 3 * DC)
                for d in range(DC):
                    own.mark(pool.tensor_scalar(mix[:, 2, d], xx[:, d], cols_sb[:, COL_XV + d:COL_XV + d + 1], None, ALU.mult))
                own.wait()
                pool.tensor_tensor(mix[:, 2], mix[:, 2], xnT[:, :, c * CH + 1:c * CH + CH + 1],
                                   ALU.add).then_inc(vmixed, 1)
                pool.wait_ge(vmixed, c + 1)

            def gather(s, r):
                own.step(pool.tensor_copy(idx_now[:, r:r + 1], idx[:, bass.ds(s, 1)]))
                pool.nop(nofuse=True)
                pool.indirect_dma_start(out=xg[:, r, :], out_offset=None, in_=xn_dram,
                                        in_offset=bass.IndirectOffsetOnAxis(ap=idx_now[:, r:r + 1], axis=0)).then_inc(
                    xg_in[r], 16)

            pool.wait_ge(xn_out, 16 * NCH)
            pool.wait_ge(idx_ok, 1)
            pool.wait_ge(route_read, 1)
            for s in range(4):
                gather(s, s)

            def step(base, f, i):
                s = base + f
                if f and (not isinstance(s, int) or s + 3 < SLOTS):
                    pool.wait_ge(gt_ps, s)
                    gather(s + 3, (f + 3) % 4)

            slot_steps(step, lambda n: own.loop(n, NS, 1))

            pool.wait_ge(y_out[0], 16 * SLOTS // 2)
            pool.wait_ge(y_out[1], 16 * SLOTS // 2)
            pool.wait_ge(sh_ps, SLOTS)

            def gather_rows(m, q):
                pool.wait_ge(combined, m * TPC + (q - 1 + ROWS_FREE))
                own.step(pool.tensor_copy(idx_now[:, q % 2 * K:q % 2 * K + K], sloti[:, bass.ds(m * -TPC + (NT - TPC + q), 1), :].rearrange("p t k -> p (t k)")))
                pool.nop(nofuse=True)
                for k in range(K):
                    pool.indirect_dma_start(
                        out=yrows[:, q % 2, k, :], out_offset=None, in_=y_dram,
                        in_offset=bass.IndirectOffsetOnAxis(ap=idx_now[:, q % 2 * K + k:q % 2 * K + k + 1], axis=0)).then_inc(
                        yrows_in[q % 2], 16)

            with own.loop(H // 2, TPC) as m:
                for v, (hh, c) in enumerate(units):
                    if v % NCH < 2:
                        gather_rows(m, 2 * hh + v % NCH)
                    for q in range(2):
                        n = first_pair[v] + 2 * c + q
                        pool.wait_ge(p_ok, m * NP + (n + 1 + SCORES_FREE))
                        pool.nop(nofuse=True)
                        for j in range(2):
                            o = (2 * q + j) * P
                            b = pr[:, n % 4, j, o:o + P]
                            mk = pool.affine_select(out=b, in_=b, compare_op=ALU.is_ge, fill=0.0, base=0,
                                                    pattern=[[1, P]], channel_multiplier=-1)
                        mk.then_inc(masked, 1)

        @block.scalar
        def _(act):
            own = Own(act, act_own)
            for t in range(NT):
                act.wait_ge(xT_ps, t + 1)
                act.activation(xnT[:, :, 1 + t * P:1 + (t + 1) * P], psum[:, t % 2, :].rearrange("p (c n) -> p c n", c=DC),
                               ACT.Copy).then_inc(xT_ok, 1)
            act.wait_ge(h1_ps, 1)
            act.wait_ge(cols_in, 16)
            for j in range(2):
                g = act.activation(h1[:, j:j + 1], psum[:, 6, j:j + 1], ACT.Gelu, bias=cols_sb[:, COL_B1 + j:COL_B1 + j + 1],
                                   scale=1.0 / N)
            g.then_inc(h1_ok, 1)

            def values(c):
                for t in range(TPC):
                    u = c * 3 * DC + 2 * DC + t
                    act.wait_ge(proj_ps, u + 1)
                    act.activation(vals[:, c * TPC + t, :].rearrange("p (h v) -> p h v", h=H)[:, :, 0:DH],
                                   psum[:, u % 4, :].rearrange("p (h v) -> p h v", h=H), ACT.Sigmoid).then_inc(v_read, 1)

            values(0)
            act.wait_ge(z_ok, 1)
            act.activation(td[:, 4:8], td[:, 0:4], ACT.Exp, bias=td[:, 8:9], accum_out=td[:, 9:10]).then_inc(z_exp, 1)
            act.wait_ge(lg_shift, 1)
            act.activation(ex, ex, ACT.Exp).then_inc(lg_exp, 1)
            for c in range(1, NCH):
                values(c)

            def tokens(s, f):
                act.wait_ge(gt_ps, s + 1)
                at_least(act, gu_ps[0], s - 1)
                act.activation(xgT[:, f % 2], psum[:, 0, :].rearrange("p (c n) -> p c n", c=DC), ACT.Copy).then_inc(xgT_ok, 1)

            def stage(i):
                act.activation(xst, xnT[:, :, bass.ds(i * P + 1, P)], ACT.Copy).then_inc(stage_ok, 1)

            def silu(kind, s):
                act.wait_ge(gu_ps[kind], s + 1)
                at_least(act, h_ok[kind], s)
                act.activation(sg[:, kind], psum[:, 1 + kind, 0:F], ACT.Silu).then_inc(silu_ok[kind], 1)

            def rows_out(y, f):
                act.wait_ge(y_ps, y + 1)
                at_least(act, y_out[f % 2], 16 * (y // 2) if isinstance(y, int) else (y - f % 2) * 8)
                act.activation(ysb[:, f % 2], psum[:, 5 + f % 2, :], ACT.Copy).then_inc(y_ok, 1)

            stage(0)
            tokens(0, 0)

            def step(base, f, i):
                s = base + f
                silu(0, s)
                if f:
                    rows_out(s - 1, f - 1)
                if not isinstance(s, int) or s + 1 < SLOTS:
                    tokens(s + 1, f + 1)
                silu(1, s)
                if f == NS - 1 and not (isinstance(i, int) and i == NT - 1):
                    stage(i + 1)

            slot_steps(step, lambda n: act.Fori(1, 1 + n))
            rows_out(SLOTS - 1, SLOTS - 1)

            act.wait_ge(y_out[0], 16 * SLOTS // 2)
            act.wait_ge(y_out[1], 16 * SLOTS // 2)
            act.wait_ge(part_out, 16 * NT)
            act.nop(nofuse=True).then_inc(p_ok, SCORES_FREE)
            with act.Fori(0, H // 2) as m:
                for n, (v, p) in enumerate(pairs):
                    o = first_column(units[v][1], p)
                    act.wait_ge(s_ps, m * NP + (n + 1))
                    act.wait_ge(pv_ps, m * NP + (n + 1))
                    act.activation(pr[:, n % 4, :, o:CH], psum[:, 2 * (n % 2):2 * (n % 2) + 2, o:CH], ACT.Exp,
                                   scale=4.0).then_inc(p_ok, 1)

        @block.tensor
        def _(pe):
            pe.wait_ge(consts, 1)
            for t in range(NT):
                pe.wait_ge(xn_ok, t + 1)
                at_least(pe, xT_ok, t - 1)
                for d in range(DC):
                    mm = pe.transpose(psum[:, t % 2, d * P:(d + 1) * P], xs[:, t, d * P:(d + 1) * P], ident[:, :])
                mm.then_inc(xT_ps, 1)
            pe.wait_ge(wr_in, 16)
            pe.wait_ge(xT_ok, NT)
            for t in range(NT):
                for d in range(DC):
                    mm = pe.matmul(psum[:, 4 + t // 8, (t % 8) * E:(t % 8 + 1) * E], xnT[:, d, 1 + t * P:1 + (t + 1) * P],
                                   wr_sb[:, d, :], start=d == 0, stop=d == DC - 1)
            mm.then_inc(lg_ps, 1)
            pe.wait_ge(te_in, 32)
            pe.wait_ge(xm_ok, 1)
            for j in range(2):
                for d in range(DC):
                    mm = pe.matmul(psum[:, 6, j:j + 1], te1_sb[:, d, j * P:(j + 1) * P], xm[:, 0, d:d + 1],
                                   start=d == 0, stop=d == DC - 1)
            mm.then_inc(h1_ps, 1)

            def project(c):
                for m in range(3):
                    pe.wait_ge(w_in[m], 16)
                    pe.wait_ge(vmixed if m == 2 else mixed[m], c + 1)
                    for n in range(DC):
                        u = c * 3 * DC + m * DC + n
                        if u >= 4:
                            v = u - 4
                            vc, vr = v // (3 * DC), v % (3 * DC)
                            if vr < 2 * DC:
                                pe.wait_ge(bits_read, vc * 2 * DC + vr + 1)
                            else:
                                pe.wait_ge(v_read, vc * TPC + vr - 2 * DC + 1)
                        for d in range(DC):
                            if m < 2:
                                mm = pe.matmul(psum[:, u % 4, :], wq_sb[:, m, d, n * P:(n + 1) * P], mix[:, m, d, :],
                                               start=d == 0, stop=d == DC - 1)
                            else:
                                mm = pe.matmul(psum[:, u % 4, :], mix[:, 2, d, n * P:(n + 1) * P], wq_sb[:, 2, d, :],
                                               start=d == 0, stop=d == DC - 1)
                        mm.then_inc(proj_ps, 1)

            project(0)
            pe.wait_ge(h1b_ok, 1)
            for j in range(2):
                mm = pe.matmul(psum[:, 7, 0:ND], h1b[:, j, :], te2_sb[:, j, :], start=j == 0, stop=j == 1)
            mm.then_inc(z_ps, 1)
            project(1)
            pe.wait_ge(onehot_ok, 1)
            for m, w in ((0, before), (1, ones_b)):
                for b in range(2):
                    for k in range(K):
                        mm = pe.matmul(psum[:, 4 + 2 * m + b, :], w[:, :], oh[:, k, b * 8:(b + 1) * 8, :].rearrange("p t e -> p (t e)"),
                                       start=k == 0, stop=k == K - 1)
                mm.then_inc(count_ps if m else rank_ps, 1)
            project(2)
            for n in range(K * NT):
                pe.wait_ge(pair_ok, n + 1)
                mm = pe.matmul(psum[:, 4, 0:P], list_a[:, n % 4, :], list_b[:, n % 4, :], start=n == 0, stop=n == K * NT - 1)
                mm.then_inc(list_ps, 1)
            pe.wait_ge(eid_ok, 1)
            pe.matmul(psum[0:1, 6, 0:P], eid[:, :], ident[:, :], start=True, stop=True).then_inc(eid_ps, 1)
            project(3)

            def transpose_tokens(s, f):
                pe.wait_ge(xg_in[f % 4], 16 * (s // 4 + 1) if isinstance(s, int) else (s - f % 4) * 4 + 16)
                at_least(pe, xgT_ok, s)
                for d in range(DC):
                    mm = pe.transpose(psum[:, 0, d * P:(d + 1) * P], xg[:, f % 4, d * P:(d + 1) * P], ident[:, :])
                mm.then_inc(gt_ps, 1)

            def up(kind, s, lhs, w):
                at_least(pe, h_ok[kind], s)
                for d in range(DC):
                    mm = pe.matmul(psum[:, 1 + kind, 0:2 * F], lhs[:, d, :], gate_up(w, d), start=d == 0, stop=d == DC - 1)
                mm.then_inc(gu_ps[kind], 1)

            def transpose_hidden(kind, s):
                pe.wait_ge(h_ok[kind], s + 1)
                at_least(pe, hT_ok[kind], s)
                pe.transpose(psum[:, 3 + kind, 0:P], hb[:, kind, :], ident[:, :]).then_inc(hT_ps[kind], 1)

            def down_expert(y, f):
                pe.wait_ge(hT_ok[0], y + 1)
                at_least(pe, y_ok, y - 1)
                pe.matmul(psum[:, 5 + f % 2, :], hT[:, 0, :], down(ew[:, f % 4]), start=True, stop=True).then_inc(y_ps, 1)

            def down_shared(y, f, tile):
                pe.wait_ge(hT_ok[1], y + 1)
                u = f % NS
                if u == 0:
                    at_least(pe, sh_read, tile)
                pe.matmul(psum[:, 7, :], hT[:, 1, :], down(sw[:, u]), start=u == 0, stop=u == NS - 1).then_inc(sh_ps, 1)

            pe.wait_ge(idx_ok, 1)
            pe.wait_ge(eidrow_ok, 1)
            pe.wait_ge(bits_read, NCH * 2 * DC)
            pe.wait_ge(v_read, NT)
            transpose_tokens(0, 0)

            def step(base, f, i):
                s = base + f
                pe.wait_ge(xgT_ok, s + 1)
                pe.wait_ge(ew_in[f % 4], 16 * (s // 4 + 1) if isinstance(s, int) else (s - f % 4) * 4 + 16)
                up(0, s, xgT[:, f % 2], ew[:, f % 4])
                if f:
                    down_expert(s - 1, f - 1)
                    transpose_hidden(1, s - 1)
                if not isinstance(s, int) or s + 1 < SLOTS:
                    transpose_tokens(s + 1, f + 1)
                u = f % NS
                tile = i if f < NS else i + 1
                if u == 0:
                    pe.wait_ge(stage_ok, tile + 1)
                pe.wait_ge(sw_in[u], 16)
                up(1, s, xst, sw[:, u])
                if f:
                    down_shared(s - 1, f - 1, i)
                transpose_hidden(0, s)

            slot_steps(step, lambda n: pe.Fori(1, 1 + n))
            down_expert(SLOTS - 1, SLOTS - 1)
            transpose_hidden(1, SLOTS - 1)
            down_shared(SLOTS - 1, SLOTS - 1, NT - 1)

            pe.wait_ge(xgT_ok, SLOTS)
            pe.nop(nofuse=True).then_inc(pv_ps, PROBS_FREE)
            with pe.Fori(0, H // 2) as m:
                def scores(n):
                    v, p = pairs[n]
                    hh, c = units[v]
                    o = first_column(c, p)
                    if n == first_pair[v] and v % NCH == 0:
                        pe.wait_ge(staged, m * 2 + (hh + 1))
                    pe.wait_ge(p_ok, m * NP + (n + 1))
                    for j in range(2):
                        mm = pe.matmul(psum[:, 2 * (n % 2) + j, o:CH], keys[:, hh, (2 * p + j) * P:(2 * p + j + 1) * P],
                                       bits[0][:, :, c * CH + o:(c + 1) * CH][:, bass.ds(m, 1), :].rearrange("p a n -> p (a n)"),
                                       start=True, stop=True)
                    mm.then_inc(s_ps, 1)

                def weighted(n):
                    v, p = pairs[n]
                    hh, c = units[v]
                    pe.wait_ge(p_ok, m * NP + (n + 1 + SCORES_FREE))
                    if p >= 2 * c:
                        pe.wait_ge(masked, m * (2 * NU) + (2 * v + p - 2 * c + 1))
                    if p == 0:
                        pe.wait_ge(oT_ok, m * NU + (v + 1))
                    for j in range(2):
                        o = max(2 * p + j - TPC * c, 0) * P
                        mm = pe.matmul(psum[0:VW, 4 + v % 2, o:CH], vst[:, hh, 2 * p + j, :], pr[:, n % 4, j, o:CH],
                                       start=2 * p + j == 0, stop=2 * p + j == TPC * (c + 1) - 1)
                    mm.then_inc(pv_ps, 1)

                def back(v):
                    pe.wait_ge(oT_ok, m * NU + (v + 1 + SUMS_FREE))
                    pe.wait_ge(o_read, m * NU + (v + 1))
                    for t in range(TPC):
                        mm = pe.transpose(psum[:, 6 + v % 2, t * VW:(t + 1) * VW], osb[:, t * P:(t + 1) * P], ident[0:VW, 0:VW])
                    mm.then_inc(o_ps, 1)

                scores(0)
                for n in range(NP):
                    if n + 1 < NP:
                        scores(n + 1)
                    weighted(n)
                    v, p = pairs[n]
                    if v and p == 1:
                        back(v - 1)
                back(NU - 1)

        @block.vector
        def _(dve):
            own = Own(dve, dve_own)

            for g in range(NCH):
                dve.wait_ge(x_in[g], 16)
                for t in range(g * TPC, (g + 1) * TPC):
                    own.mark(dve.bn_stats(stats[:, t, :], xs[:, t, :]))
                own.wait()
                for t in range(g * TPC, (g + 1) * TPC):
                    own.mark(dve.bn_aggr(mv[:, t, :], stats[:, t, :]))
                own.wait()
                v = mv[:, g * TPC:(g + 1) * TPC, 1]
                dve.tensor_scalar(v, v, EPS, None, ALU.add).then_inc(var_eps, 1)
                if g:
                    normalise(dve, g - 1, rstd_ok, xn_ok, xs, mv, rstd)
            normalise(dve, NCH - 1, rstd_ok, xn_ok, xs, mv, rstd)
            for g in range(NCH):
                dve.wait_ge(xT_ok, (g + 1) * TPC)
                own.mark(dve.tensor_reduce(xm[:, g, :], xnT[:, :, 1 + g * CH:1 + (g + 1) * CH], AX_X, ALU.add))
            own.wait()
            own.step(dve.tensor_tensor(xm[:, 0:2, :], xm[:, 0:2, :], xm[:, 2:4, :], ALU.add))
            dve.tensor_tensor(xm[:, 0, :], xm[:, 0, :], xm[:, 1, :], ALU.add).then_inc(xm_ok, 1)

            def shift_mix(m, c):
                dve.wait_ge(xx_ok, c + 1)
                if c:
                    dve.wait_ge(proj_ps, (c - 1) * 3 * DC + (m + 1) * DC)
                for d in range(DC):
                    ins = dve.scalar_tensor_tensor(mix[:, m, d], xx[:, d], cols_sb[:, m * DC + d:m * DC + d + 1],
                                                   xnT[:, d, c * CH + 1:(c + 1) * CH + 1], ALU.mult, ALU.add)
                ins.then_inc(mixed[m], 1)

            def trigger(m, c):
                for n in range(DC):
                    u = c * 3 * DC + m * DC + n
                    dve.wait_ge(proj_ps, u + 1)
                    own.mark(dve.tensor_scalar(low, psum[:, u % 4, :], THRESHOLD, 0.5, ALU.is_gt, ALU.subtract))
                    dve.tensor_scalar(high, psum[:, u % 4, :], -THRESHOLD, 0.5, ALU.is_ge, ALU.subtract).then_inc(bits_read, 1)
                    dve.wait_ge(bits_read, c * 2 * DC + m * DC + n + 1)
                    own.wait()
                    own.step(dve.tensor_tensor_scan(bits[m][:, n, c * CH:(c + 1) * CH], high, low,
                                                    bits[m][:, n, c * CH - 1:c * CH] if c else -0.5, ALU.min, ALU.max))

            dve.wait_ge(cols_in, 16)
            shift_mix(0, 0)
            shift_mix(1, 0)
            dve.wait_ge(h1_ok, 1)
            for j in range(2):
                ins = dve.tensor_copy(h1b[:, j, :], h1[:, j:j + 1].to_broadcast([P, P]))
            ins.then_inc(h1b_ok, 1)
            for m in range(2):
                trigger(m, 0)
                shift_mix(m, 1)

            dve.wait_ge(z_ps, 1)
            dve.wait_ge(rows_in, 16)
            own.step(dve.tensor_tensor(td[:, 0:4], psum[:, 7, 0:ND], rows_sb[:, ROW_B2:ROW_B2 + ND], ALU.add))
            own.step(dve.tensor_reduce(td[:, 10:11], td[:, 0:4], AX_X, ALU.max))
            dve.tensor_scalar(td[:, 8:9], td[:, 10:11], -1.0, None, ALU.mult).then_inc(z_ok, 1)
            dve.wait_ge(z_exp, 1)
            own.step(dve.reciprocal(td[:, 11:12], td[:, 9:10]))
            own.step(dve.tensor_scalar(td[:, 12:16], td[:, 4:8], td[:, 11:12], 0.5, ALU.mult, ALU.mult))
            aff = rows_sb[:, ROW_AFF:ROW_AFF + ND * E].rearrange("p (n e) -> p n e", n=ND)
            own.step(dve.tensor_scalar(dom[:, :], aff[:, 0], td[:, 12:13], None, ALU.mult))
            for n in range(1, ND):
                own.step(dve.scalar_tensor_tensor(dom[:, :], aff[:, n], td[:, 12 + n:13 + n], dom[:, :], ALU.mult, ALU.add))
            dve.wait_ge(lg_ps, 1)
            dve.wait_ge(xn_out, 16 * NCH)
            dve.wait_ge(xT_ps, NT)
            own.step(dve.tensor_tensor(lg, psum[:, 4:6, :].rearrange("p b (t e) -> p (b t) e", e=E),
                                       dom[:, :].unsqueeze(1).to_broadcast([P, NT, E]), ALU.add))
            own.mark(dve.tensor_tensor(lb, lg, rows_sb[:, ROW_RB:ROW_RB + E].unsqueeze(1).to_broadcast([P, NT, E]), ALU.add))
            own.step(dve.tensor_reduce(mx[:, :], lg, AX_X, ALU.max))
            dve.tensor_tensor(ex, lg, mx[:, :].unsqueeze(2).to_broadcast([P, NT, E]), ALU.subtract).then_inc(lg_shift, 1)
            for t in range(NT):
                own.mark(dve.max(top[:, t, :], lb[:, t, :]))
            own.wait()
            for t in range(NT):
                own.mark(dve.max_index(topi[:, t, :], top[:, t, :], lb[:, t, :]))
            own.wait()
            own.step(dve.tensor_copy(topf[:, :, :], topi[:, :, 0:K]))
            for k in range(K):
                ins = dve.tensor_tensor(oh[:, k], iota_e[:, :].unsqueeze(1).to_broadcast([P, NT, E]),
                                        topf[:, :, k:k + 1].to_broadcast([P, NT, E]), ALU.is_equal)
            ins.then_inc(onehot_ok, 1)
            for m in range(2):
                trigger(m, 1)
                shift_mix(m, 2)

            dve.wait_ge(onehot_ok, 1)
            dve.wait_ge(lg_exp, 1)
            own.step(dve.tensor_reduce(zs[:, :], ex, AX_X, ALU.add))
            own.step(dve.reciprocal(zs[:, :], zs[:, :]))
            for k in range(K):
                own.step(dve.tensor_tensor(prod, oh[:, k], ex, ALU.mult))
                own.step(dve.tensor_reduce(wgt[:, k, :], prod, AX_X, ALU.add))
            own.step(dve.tensor_tensor(wgt[:, :, :], wgt[:, :, :], zs[:, :].unsqueeze(1).to_broadcast([P, K, NT]), ALU.mult))
            own.step(dve.tensor_reduce(wsum[:, :], wgt[:, :, :].rearrange("p k t -> p t k"), AX_X, ALU.add))
            own.step(dve.tensor_scalar(wsum[:, :], wsum[:, :], 1e-8, None, ALU.add))
            own.step(dve.reciprocal(wsum[:, :], wsum[:, :]))
            own.step(dve.tensor_tensor(wgt[:, :, :], wgt[:, :, :], wsum[:, :].unsqueeze(1).to_broadcast([P, K, NT]), ALU.mult))
            dve.wait_ge(count_ps, 1)
            counts = psum[:, 6:8, :].rearrange("p b (t e) -> p (b t) e", e=E)
            own.step(dve.tensor_scalar(cum[:, 0, :], counts[:, 0, :], 0.0, None, ALU.mult))
            for t in range(NT - 1):
                own.step(dve.tensor_tensor(cum[:, t + 1, :], counts[:, t, :], cum[:, t, :], ALU.add))
            own.step(dve.tensor_tensor(cnt[:, :], counts[:, NT - 1, :], cum[:, NT - 1, :], ALU.add))
            own.step(dve.tensor_scalar(cnti[:, :], cnt[:, :], float(P - 1), None, ALU.add))
            own.step(dve.tensor_scalar(cnti[:, :], cnti[:, :], 7, None, ALU.arith_shift_right))
            own.step(dve.tensor_copy(cnt[:, :], cnti[:, :]))
            own.step(dve.tensor_tensor_scan(incl[:, :], ones_e[:, :], cnt[:, :], 0.0, ALU.mult, ALU.add))
            own.step(dve.tensor_tensor(cnt[:, :], incl[:, :], cnt[:, :], ALU.subtract))
            own.step(dve.tensor_scalar(cnt[:, :], cnt[:, :], float(P), None, ALU.mult))
            own.step(dve.tensor_scalar(dom[:, :], incl[:, :], part_i[:, :], None, ALU.is_le, ALU.add, accum_out=eid[:, :]))
            dve.tensor_scalar(eid[:, :], eid[:, :], float(E - 1), None, ALU.min).then_inc(eid_ok, 1)
            dve.wait_ge(rank_ps, 1)
            own.step(dve.tensor_tensor(pos, psum[:, 4:6, :].rearrange("p b (t e) -> p (b t) e", e=E), cum, ALU.add))
            own.step(dve.tensor_tensor(pos, pos, cnt[:, :].unsqueeze(1).to_broadcast([P, NT, E]), ALU.add))
            for k in range(K):
                own.step(dve.tensor_tensor(prod, oh[:, k], pos, ALU.mult))
                own.step(dve.tensor_reduce(slotf[:, k, :], prod, AX_X, ALU.add))
            own.mark(dve.tensor_copy(hii[:, :, :], slotf[:, :, :]))
            dve.tensor_copy(sloti[:, :, :], slotf[:, :, :].rearrange("p k t -> p t k")).then_inc(route_read, 1)
            own.wait()
            own.step(dve.tensor_scalar(hii[:, :, :], hii[:, :, :], 7, None, ALU.arith_shift_right))
            own.step(dve.tensor_copy(hif[:, :, :], hii[:, :, :]))
            own.step(dve.scalar_tensor_tensor(lof[:, :, :], hif[:, :, :], -float(P), slotf[:, :, :], ALU.mult, ALU.add))

            def pair(n):
                t, k = n // K, n % K
                at_least(dve, list_ps, n - 3)
                dve.tensor_scalar(list_a[:, n % 4, :], iota_s[:, :], lof[:, k, t:t + 1], None, ALU.is_equal)
                dve.tensor_scalar(list_b[:, n % 4, :], iota_s[:, :], hif[:, k, t:t + 1], tok_i[:, t:t + 1],
                                  ALU.is_equal, ALU.mult).then_inc(pair_ok, 1)

            for m in range(2):
                trigger(m, 2)
                shift_mix(m, 3)
            for n in range(K * NT):
                pair(n)
            dve.wait_ge(list_ps, K * NT)
            dve.tensor_copy(idx[:, :], psum[:, 4, 0:P]).then_inc(idx_ok, 1)
            dve.wait_ge(eid_ps, 1)
            dve.tensor_copy(eid_row[:, :], psum[0:1, 6, 0:P]).then_inc(eidrow_ok, 1)
            for m in range(2):
                trigger(m, 3)

            def hidden(kind, s):
                dve.wait_ge(silu_ok[kind], s + 1)
                at_least(dve, hT_ps[kind], s)
                dve.tensor_tensor(hb[:, kind], psum[:, 1 + kind, F:2 * F], sg[:, kind], ALU.mult).then_inc(h_ok[kind], 1)

            def hidden_T(kind, s):
                dve.wait_ge(hT_ps[kind], s + 1)
                at_least(dve, y_ps if kind == 0 else sh_ps, s)
                dve.tensor_copy(hT[:, kind], psum[:, 3 + kind, 0:P]).then_inc(hT_ok[kind], 1)

            def shared_out(i):
                dve.wait_ge(sh_ps, (i + 1) * NS)
                dve.wait_ge(xt_in, 16 * (i + 1))
                at_least(dve, part_out, 16 * i)
                dve.tensor_tensor(psh, psum[:, 7, :], xt, ALU.add).then_inc(sh_read, 1)
                dve.wait_ge(sh_read, i + 1)
                dve.tensor_tensor(psh, psh, rows_sb[:, ROW_E0:ROW_E0 + D], ALU.add).then_inc(part_ok, 1)

            def step(base, f, i):
                s = base + f
                hidden(0, s)
                if f:
                    hidden_T(1, s - 1)
                hidden(1, s)
                if f == NS:
                    shared_out(i)
                hidden_T(0, s)

            slot_steps(step, lambda n: dve.Fori(1, 1 + n))
            hidden_T(1, SLOTS - 1)
            shared_out(NT - 1)

            dve.wait_ge(gu_ps[1], SLOTS)
            dve.wait_ge(stage_ok, NT)
            for hh in range(2):
                dve.memset(keys[DH - DH * hh:2 * DH - DH * hh, hh, :].bitcast(U32), 0)

            def stage(m, hh):
                rows_ = slice(DH * hh, DH * hh + DH)
                dve.tensor_copy(keys[rows_, hh, :], bits[1][rows_, bass.ds(m, 1), :].rearrange("p a n -> p (a n)"))
                dve.tensor_copy(vst[:, hh], vals[:, :, bass.ds(m * (2 * VW) + hh * VW, VW)]).then_inc(staged, 1)

            stage(0, 0)
            stage(0, 1)
            own.step(dve.tensor_tensor(rows_sb[:, ROW_E1:ROW_E1 + D], rows_sb[:, ROW_E1:ROW_E1 + D],
                                       rows_sb[:, ROW_E0:ROW_E0 + D], ALU.subtract))
            dve.nop(nofuse=True).then_inc(oT_ok, SUMS_FREE)
            dve.nop(nofuse=True).then_inc(o_read, SUMS_FREE)
            dve.nop(nofuse=True).then_inc(o_ps, 1)
            dve.nop(nofuse=True).then_inc(combined, ROWS_FREE)
            for c in chunks:
                dve.wait_ge(acc_in[c], 16)

            def combine(m, q):
                tile = m * -TPC + (NT - TPC + q)
                dve.wait_ge(yrows_in[q % 2], m * (16 * K * 2) + 16 * K * (q // 2 + 1))
                dst = acc[:, bass.ds(tile, 1), :].rearrange("p a d -> p (a d)")
                for k in range(K):
                    ins = dve.scalar_tensor_tensor(dst, yrows[:, q % 2, k, :], wgt[:, k, bass.ds(tile, 1)], dst, ALU.mult, ALU.add)
                    if k < K - 1:
                        own.step(ins)
                ins.then_inc(combined, 1)
                dve.wait_ge(combined, m * TPC + (q + 1 + ROWS_FREE))

            with own.loop(H // 2, NU * 2 + TPC * (K - 1)) as m:
                for v, (hh, c) in enumerate(units):
                    dve.wait_ge(pv_ps, m * NP + (last_of(v) + PROBS_FREE))
                    dve.wait_ge(o_ps, m * NU + (v + 1))
                    dve.tensor_copy(osb, psum[0:VW, 4 + v % 2, :]).then_inc(oT_ok, 1)
                    if v % NCH == NCH - 1:
                        stage((m + 1) % (H // 2), hh)
                    if v % NCH in (1, 2):
                        dve.wait_ge(unit_ok, m * NU + v)
                        combine(m, 2 * hh + v % NCH - 1)
                    dve.wait_ge(o_ps, m * NU + (v + 2))
                    o = psum[:, 6 + v % 2, 0:TPC * VW].rearrange("p (t v) -> p t v", v=VW)
                    own.step(dve.reciprocal(rden, o[:, :, DH]))
                    dve.tensor_tensor(xo, o[:, :, 0:DH], rden.unsqueeze(2).to_broadcast([P, TPC, DH]), ALU.mult).then_inc(o_read, 1)
                    dve.wait_ge(o_read, m * NU + (v + 1 + SUMS_FREE))
                    own.step(dve.tensor_tensor(
                        xo, xo, rows_sb[:, bass.ds(m * (2 * DH) + (ROW_E1 + hh * DH), DH)].unsqueeze(1).to_broadcast([P, TPC, DH]),
                        ALU.mult))
                    dst = acc[:, c * TPC:(c + 1) * TPC, bass.ds(m * (2 * DH) + hh * DH, DH)]
                    dve.tensor_tensor(dst, dst, xo, ALU.add).then_inc(unit_ok, 1)


def normalise(dve, g, rstd_ok, xn_ok, xs, mv, rstd):
    dve.wait_ge(rstd_ok, g + 1)
    for t in range(g * TPC, (g + 1) * TPC):
        dve.tensor_scalar(xs[:, t, :], xs[:, t, :], mv[:, t, 0:1], rstd[:, t:t + 1], ALU.subtract, ALU.mult).then_inc(xn_ok, 1)


def kernel(**inputs):
    import numpy as np
    import concourse.bacc as bacc
    from concourse.bass_utils import run_bass_kernel_spmd

    def get(name):
        return np.asarray(inputs[name])

    def rows_to_partitions(w):
        return w.reshape(DC, P, w.shape[1]).transpose(1, 0, 2)

    def unit_weights(gate, up, down):
        u = gate.shape[0]
        gu = np.stack([gate.reshape(u, DC, P, F), up.reshape(u, DC, P, F)], axis=3)
        gu = gu.transpose(0, 2, 1, 3, 4).reshape(u, P, DC * 2 * F)
        return np.concatenate([gu, down], axis=2)

    def split_shared(w):
        return w.reshape(2, D, NS // 2, F).transpose(0, 2, 1, 3).reshape(NS, D, F)

    def by_partition(v):
        return v.reshape(-1, P).T

    arrays = {
        "x": get("L0_attn_x").reshape(N, D),
        "wqkv": np.stack([rows_to_partitions(get(n).T) for n in ("L0_attn_Wq", "L0_attn_Wk", "L0_attn_Wv")]),
        "cols": np.concatenate([by_partition(get(n)) for n in ("L0_attn_x_q", "L0_attn_x_k", "L0_attn_x_v", "L0_ffn_te_b1")], axis=1),
        "rows": np.concatenate([get("L0_attn_emb0").reshape(-1), get("L0_attn_emb1").reshape(-1), get("L0_ffn_affinity").T.reshape(-1),
                                get("L0_ffn_router_bias"), get("L0_ffn_te_b2")]).reshape(1, ROW_COLS),
        "wr": rows_to_partitions(get("L0_ffn_Wr").T),
        "te1": rows_to_partitions(get("L0_ffn_te_W1").T),
        "te2": get("L0_ffn_te_W2").T.reshape(2, P, ND).transpose(1, 0, 2),
        "wshared": unit_weights(split_shared(get("L0_ffn_Sg")), split_shared(get("L0_ffn_Su")), get("L0_ffn_Sd").reshape(NS, F, D)),
        "wexperts": unit_weights(get("L0_ffn_Wg"), get("L0_ffn_Wu"), get("L0_ffn_Wd")),
    }
    arrays = {n: np.ascontiguousarray(a) for n, a in arrays.items()}
    nc = bacc.Bacc("TRN2", target_bir_lowering=False, num_devices=1)
    aps = [nc.dram_tensor(n, a.shape, mybir.dt.from_np(a.dtype), kind="ExternalInput").ap() for n, a in arrays.items()]
    aps.append(nc.dram_tensor("out", (N, D), F32, kind="ExternalOutput").ap())
    build(nc, *aps)
    r = run_bass_kernel_spmd(nc, [arrays], core_ids=[0])
    return r.results[0]["out"].reshape(1, N, D)
```

```python
from contextlib import ExitStack, contextmanager

import concourse.bass as bass
from concourse import mybir

ALU = mybir.AluOpType
ACT = mybir.ActivationFunctionType
AX_X = mybir.AxisListType.X
F32 = mybir.dt.float32
F32R = mybir.dt.float32r
BF16 = mybir.dt.bfloat16
F16 = mybir.dt.float16
I32 = mybir.dt.int32
U32 = mybir.dt.uint32

P = 128
N = 2048
D = 512
DC = D // P
NT = N // P
CH = 512
NCH = N // CH
TPC = CH // P
H = 8
DH = D // H
VW = DH + 1
E = 64
K = 4
F = 128
NS = 8
SLOTS = NT * NS
SCORES_FREE, PROBS_FREE, SUMS_FREE, ROWS_FREE = 2, 4, 2, 2
LIST_SHARE = [[5] * DC, [5] * DC, [8, 8, 8, 0]]
assert sum(map(sum, LIST_SHARE)) == K * NT
WCOLS = DC * 2 * F + D
EPS = 1e-5
THRESHOLD = 0.001
MASKED = -64.0
ND = 4
assert (K * N + E * (P - 1)) // P <= SLOTS <= P

ROW_E0, ROW_E1, ROW_AFF, ROW_RB, ROW_B2 = 0, D, 2 * D, 2 * D + ND * E, 2 * D + ND * E + E
ROW_COLS = ROW_B2 + ND
COL_XQ, COL_XK, COL_XV, COL_B1 = 0, DC, 2 * DC, 3 * DC
COL_COLS = COL_B1 + 2


def at_least(eng, sem, value):
    if not (isinstance(value, int) and value <= 0):
        eng.wait_ge(sem, value)


class Own:

    def __init__(self, eng, sem):
        self.eng, self.sem, self.base, self.n = eng, sem, 0, 0

    def mark(self, ins):
        ins.then_inc(self.sem, 1)
        self.n += 1

    def wait(self):
        self.eng.wait_ge(self.sem, self.base + self.n)

    def step(self, ins):
        self.mark(ins)
        self.wait()

    @contextmanager
    def loop(self, trips, per_trip, first=0):
        outer = self.base + self.n
        with self.eng.Fori(first, first + trips) as i:
            self.base, self.n = outer - first * per_trip + i * per_trip, 0
            yield i
            assert self.n == per_trip, self.n
        self.base, self.n = outer + trips * per_trip, 0


def list_share(m, n):
    share = [LIST_SHARE[m][j] for m in range(3) for j in range(DC)]
    first = sum(share[:m * DC + n])
    return range(first, first + share[m * DC + n])


def slot_steps(step, loop):
    for f in range(NS + 1):
        step(0, f, 0)
    with loop(NT - 2) as i:
        for f in range(1, NS + 1):
            step(i * NS, f, i)
    for f in range(1, NS):
        step((NT - 1) * NS, f, NT - 1)


def build(nc, x, wqkv, cols, rows, wr, te1, te2, wshared, wexperts, out):
    with ExitStack() as ctx:
        def sb(name, shape, dt=F32, phase=ctx):
            return phase.enter_context(nc.sbuf_tensor(name, shape, dt))

        def sem(name):
            return ctx.enter_context(nc.semaphore(name))

        xn_dram = nc.dram_tensor("xn_dram", [N, D], F32, kind="Internal").ap()
        part_dram = nc.dram_tensor("part_dram", [NT, P, D], F32, kind="Internal").ap()
        y_dram = nc.dram_tensor("y_dram", [SLOTS * P, D], F32, kind="Internal").ap()
        xT_dram = nc.dram_tensor("xT_dram", [NT, P, DC, P], F32, kind="Internal").ap()
        q_dram = nc.dram_tensor("q_dram", [D, N], BF16, kind="Internal").ap()
        k_dram = nc.dram_tensor("k_dram", [D, N], BF16, kind="Internal").ap()
        v_dram = nc.dram_tensor("v_dram", [H, P, NT, VW], F32, kind="Internal").ap()
        y_slots = y_dram.rearrange("(s p) d -> s p d", p=P)

        rows_sb = sb("rows_sb", [P, ROW_COLS])
        cols_sb = sb("cols_sb", [P, COL_COLS])
        te2_sb = sb("te2_sb", [P, 2, ND])
        ident = sb("ident", [P, P])
        iota_e = sb("iota_e", [P, E])
        iota_s = sb("iota_s", [P, P], F16)
        tok_i = sb("tok_i", [P, NT])
        part_i = sb("part_i", [P, 1])
        before = sb("before", [P, P], BF16)
        ones_b = sb("ones_b", [P, P], BF16)
        masked_b = sb("masked_b", [P, P], BF16)
        stats = sb("stats", [P, NT, 6])
        mv = sb("mv", [P, NT, 2])
        mhalf = sb("mhalf", [P, TPC])
        rstd = sb("rstd", [P, NT])
        xm = sb("xm", [P, NCH, DC])
        h1 = sb("h1", [P, 2])
        td = sb("td", [P, 16])
        dom = sb("dom", [P, E])
        mx = sb("mx", [P, NT])
        zs = sb("zs", [P, NT])
        top = sb("top", [P, NT, 8])
        topi = sb("topi", [P, NT, 8], U32)
        topf = sb("topf", [P, NT, K])
        wgt = sb("wgt", [P, K, NT])
        wsum = sb("wsum", [P, NT])
        cnt = sb("cnt", [P, E])
        cnti = sb("cnti", [P, E], I32)
        incl = sb("incl", [P, E])
        ones_e = sb("ones_e", [P, E])
        eid = sb("eid", [P, 1])
        eid_row = sb("eid_row", [1, SLOTS], I32)
        slotf = sb("slotf", [P, K, NT])
        sloti = sb("sloti", [P, NT, K], U32)
        hii = sb("hii", [P, K, NT], I32)
        hif = sb("hif", [P, K, NT])
        lof = sb("lof", [P, K, NT])
        idx = sb("idx", [P, SLOTS], U32)
        idx_now = sb("idx_now", [P, 2 * K], U32)
        psum = ctx.enter_context(nc.psum_tensor("psum", [P, 8, CH], F32))

        with ExitStack() as front:
            reg_b = sb("reg_b", [P, NT * D], phase=front)
            reg_c = sb("reg_c", [P, 4608], phase=front)
            XW = N + 8
            xnT = sb("xnT", [P, DC, XW], phase=front)
            w_r = [sb(f"w_r{m}", [P, 2, DC, D], F32R, front) for m in range(3)]
            mix_r = [sb(f"mix_r{b}", [P, 2, DC, CH], F32R, front) for b in range(2)]
            mraw = [sb(f"mraw{b}", [P, DC, CH], phase=front) for b in range(2)]
            bits = [sb("qbits", [P, DC, CH], BF16, front), sb("kbits", [P, DC, CH], BF16, front)]
            vals = sb("vals", [P, H, TPC, VW], phase=front)
        with ExitStack() as early:
            for name, shape, dt in (("reg_b_", [P, NT * D], F32), ("reg_c_", [P, 4608], F32), ("xnT_", [P, DC, XW], F32),
                                    ("w_r_", [P, 6 * DC * D], F32), ("mix_r_", [P, 4 * DC * CH], F32), ("mraw_", [P, 2 * DC * CH], F32)):
                sb(name, shape, dt, early)
            wv_raw = sb("wv_raw", [P, DC, D], phase=early)
            wk_raw = sb("wk_raw", [P, DC, D], phase=early)
        w_raw = [mraw[1], wk_raw, wv_raw]
        with ExitStack() as early:
            for name, shape, dt in (("reg_b__", [P, NT * D], F32), ("reg_c__", [P, 4608], F32), ("xnT__", [P, DC, XW], F32),
                                    ("w_r__", [P, 6 * DC * D], F32), ("mix_r__", [P, 4 * DC * CH], F32), ("mraw__", [P, 2 * DC * CH], F32),
                                    ("wv_raw__", [P, DC, D], F32)):
                sb(name, shape, dt, early)
            te1_t = sb("te1_t", [P, DC, 2 * P], phase=early)
        te1_sb = te1_t[:, :, :]
        xs = reg_b[:, :].rearrange("p (t d) -> p t d", t=NT)
        lg = reg_b[:, 0:1024].rearrange("p (t e) -> p t e", t=NT)
        lb = reg_b[:, 1024:2048].rearrange("p (t e) -> p t e", t=NT)
        ex = reg_b[:, 2048:3072].rearrange("p (t e) -> p t e", t=NT)
        pos = reg_b[:, 3072:4096].rearrange("p (t e) -> p t e", t=NT)
        prod = reg_b[:, 4096:5120].rearrange("p (t e) -> p t e", t=NT)
        oh = reg_b[:, 5120:7168].bitcast(BF16).rearrange("p (k t e) -> p k t e", k=K, t=NT)
        cum = reg_b[:, 7168:8192].rearrange("p (t e) -> p t e", t=NT)
        shift = reg_c[:, 0:DC * CH].rearrange("p (c n) -> p c n", c=DC)
        wr_sb = reg_c[:, 3584:3840].rearrange("p (c n) -> p c n", c=DC)
        h1b = reg_c[:, 3840:4096].rearrange("p (j n) -> p j n", j=2)
        qk = reg_c[:, 2560:3584].rearrange("p (r n) -> p r n", r=2)
        list_a = reg_c[:, 2048:2560].bitcast(F16).rearrange("p (r n) -> p r n", r=8)
        list_b = reg_c[:, 3584:4096].bitcast(F16).rearrange("p (r n) -> p r n", r=8)
        low, high = reg_c[:, 4096:4352].bitcast(BF16), reg_c[:, 4352:4608].bitcast(BF16)

        with ExitStack() as middle:
            sraw = sb("sraw", [P, 2 * WCOLS + 16], phase=middle)
            eraw = sb("eraw", [P, 4, WCOLS], phase=middle)
            xg = sb("xg", [P, 4, D], phase=middle)
            ew_r = [sb(f"ew_r{b}", [P, 2, WCOLS], F32R, middle) for b in range(2)]
            xT_r = sb("xT_r", [P, 2, 2, DC, P], F32R, middle)
            xst_r = sb("xst_r", [P, 2, DC, P], F32R, middle)
            xtile = sb("xtile", [P, DC, P], phase=middle)
            h_r = sb("h_r", [P, 2, 2, P], F32R, middle)
            hb = sb("hb", [P, 2, F], phase=middle)
            sg = sb("sg", [P, 2, F], phase=middle)
            ysb = sb("ysb", [P, 2, D], phase=middle)
            psh = sb("psh", [P, D], phase=middle)
            xt = sb("xt", [P, D], phase=middle)
            sw_r = sb("sw_r", [P, NS, 2, WCOLS], F32R, middle)

        with ExitStack() as end:
            keys = sb("keys", [DH, 2, N], BF16, end)
            queries = sb("queries", [DH, 2, N], BF16, end)
            vraw = sb("vraw", [P, 2, NT, VW], phase=end)
            pf = sb("pf", [P, 4, 2, CH], phase=end)
            ph = sb("ph", [P, 4, 2, CH], F32R, end)
            pl = sb("pl", [P, 4, 2, CH], F32R, end)
            v_r = [sb(f"v_r{hh}", [P, 2, NT, VW], F32R, end) for hh in range(2)]
            osb = sb("osb", [VW, 2, CH], phase=end)
            xo = sb("xo", [P, TPC, DH], phase=end)
            rden = sb("rden", [P, TPC], phase=end)
            acc = sb("acc", [P, NT, D], phase=end)
            yrows = sb("yrows", [P, K, D], phase=end)
            ysum = sb("ysum", [P, 2, D], phase=end)

        def gate_up(w, c):
            return w[:, c * 2 * F:(c + 1) * 2 * F]

        def down(w):
            return w[:, DC * 2 * F:WCOLS]

        UP, DOWN, ALL = slice(0, DC * 2 * F), slice(DC * 2 * F, WCOLS), slice(0, WCOLS)

        def as_f32(ap):
            return ap.bitcast(F32)

        x_in = [sem(f"x_in{g}") for g in range(NCH)]
        rows_in, cols_in, te_in, wr_in = sem("rows_in"), sem("cols_in"), sem("te_in"), sem("wr_in")
        w_in = [sem(f"w_in{m}") for m in range(3)]
        dve_own, act_own, pool_own = sem("dve_own"), sem("act_own"), sem("pool_own")
        consts = sem("consts")
        var_eps, rstd_ok, xn_ok, xn_out = sem("var_eps"), sem("rstd_ok"), sem("xn_ok"), sem("xn_out")
        xT_ps, xT_ok, xm_ok = sem("xT_ps"), sem("xT_ok"), sem("xm_ok")
        lg_ps, h1_ps, h1_ok, h1b_ok, z_ps, z_ok, z_exp = (sem(n) for n in (
            "lg_ps", "h1_ps", "h1_ok", "h1b_ok", "z_ps", "z_ok", "z_exp"))
        lg_shift, lg_exp, onehot_ok, rank_ps, count_ps = (sem(n) for n in (
            "lg_shift", "lg_exp", "onehot_ok", "rank_ps", "count_ps"))
        pair_ok, list_ps, eid_ok, eid_ps, idx_ok, eidrow_ok, route_read = (sem(n) for n in (
            "pair_ok", "list_ps", "eid_ok", "eid_ps", "idx_ok", "eidrow_ok", "route_read"))
        qk_read = sem("qk_read")
        shift_ok = sem("shift_ok")
        mixed, mix_high, mix_low = [sem(f"mixed{m}") for m in range(3)], sem("mix_high"), sem("mix_low")
        w_high, w_low = [sem(f"w_high{m}") for m in range(3)], [sem(f"w_low{m}") for m in range(3)]
        ones_ok, te2_in = sem("ones_ok"), sem("te2_in")
        scale_ok, v_scaled = sem("scale_ok"), [sem("v_scaled0"), sem("v_scaled1")]
        proj_ps, bits_read, v_read = sem("proj_ps"), sem("bits_read"), sem("v_read")
        sw_in = [sem(f"sw_in{b}") for b in range(2)]
        ew_in = [sem(f"ew_in{r}") for r in range(4)]
        xg_in = [sem(f"xg_in{r}") for r in range(4)]
        bits_ok, bits_out, v_out = sem("bits_ok"), sem("bits_out"), sem("v_out")
        xT_out, xtile_in, gt_ps = sem("xT_out"), sem("xtile_in"), sem("gt_ps")
        x_high, x_low, st_high, st_low = sem("x_high"), sem("x_low"), sem("st_high"), sem("st_low")
        eup_exp, eup_low, edn_high, edn_low = sem("eup_exp"), sem("eup_low"), sem("edn_high"), sem("edn_low")
        sw_high, sw_low = sem("sw_high"), sem("sw_low")
        gu_ps, silu_ok, h_ok, hT_ps, hT_high, hT_low = ([sem(f"{n}_moe"), sem(f"{n}_shared")] for n in (
            "gu_ps", "silu_ok", "h_ok", "hT_ps", "hT_high", "hT_low"))
        y_ps, y_ok, y_out = sem("y_ps"), sem("y_ok"), [sem("y_out0"), sem("y_out1")]
        sh_ps, part_ok, part_out, xt_in = sem("sh_ps"), sem("part_ok"), sem("part_out"), sem("xt_in")
        sh_read = sem("sh_read")
        head_in = [sem("head_in0"), sem("head_in1")]
        acc_in, combined = [sem(f"acc_in{c}") for c in range(NCH)], sem("combined")
        v_high, v_low = [sem("v_high0"), sem("v_high1")], [sem("v_low0"), sem("v_low1")]
        yrows_in, rows_added = sem("yrows_in"), sem("rows_added")
        s_ps, p_exp, p_low, pv_ps, oT_ok, o_ps, o_read, unit_ok, fin_out = (sem(n) for n in (
            "s_ps", "p_exp", "p_low", "pv_ps", "oT_ok", "o_ps", "o_read", "unit_ok", "fin_out"))

        block = ctx.enter_context(nc.Block())
        chunks = list(range(NCH))[::-1]
        units = [(hh, c) for hh in range(2) for c in chunks]
        pairs = [(v, p) for v, (_, c) in enumerate(units) for p in range(2 * (c + 1))]
        NU, NP = len(units), len(pairs)
        first_pair = [min(n for n, (w, _) in enumerate(pairs) if w == v) for v in range(NU)]

        def last_of(v):
            return first_pair[v] + 2 * (units[v][1] + 1)

        def later(steps, v):
            n = last_of(v) + steps
            return n % NP, n >= NP

        SUMS, BACK, ADD = 3, 3, 6
        AHEAD = 3
        ROW_STEPS = (12, 22, 31, 37)
        VALUES_STEPS = (33, 16)
        LEAD = ADD + 1

        def rounds(part, loop):
            part(0, 0, LEAD, None)
            with loop(H // 2 - 1) as m:
                part(m, LEAD, NP, None)
                part(m + 1, 0, LEAD, m)
            part(H // 2 - 1, LEAD, NP, None)

        def low_and_high(n):
            return n % 5 == 2

        def first_column(c, p):
            return CH // 2 if p == 2 * c + 1 else 0

        @block.sync
        def _(sp):
            xv = x.rearrange("(t p) d -> p t d", p=P)
            for g in range(NCH):
                if g == 1:
                    sp.dma_start(wr_sb, wr).then_inc(wr_in, 16)
                    sp.dma_start(cols_sb[:, :], cols).then_inc(cols_in, 16)
                if g == 2:
                    sp.dma_start(w_raw[0][:, :, :], wqkv[0]).then_inc(w_in[0], 16)
                sp.dma_start(xs[:, g * TPC:(g + 1) * TPC, :], xv[:, g * TPC:(g + 1) * TPC, :]).then_inc(x_in[g], 16)
            sp.dma_start(te2_sb[:, :, :], te2).then_inc(te2_in, 16)
            for m in range(1, 3):
                sp.dma_start(w_raw[m][:, :, :], wqkv[m]).then_inc(w_in[m], 16)
            sp.dma_start(rows_sb[:, :], rows.to_broadcast([P, ROW_COLS])).then_inc(rows_in, 16)
            xnv = xn_dram.rearrange("(t p) d -> p t d", p=P)
            for g in range(NCH):
                sp.wait_ge(xn_ok, (g + 1) * TPC)
                sp.dma_start(xnv[:, g * TPC:(g + 1) * TPC, :], xs[:, g * TPC:(g + 1) * TPC, :]).then_inc(xn_out, 16)

            sp.wait_ge(w_low[1], 1)
            sp.dma_start(te1_sb, te1).then_inc(te_in, 16)

            def load_expert(s, r):
                e = sp.value_load(eid_row[0:1, bass.ds(s, 1)], min_val=0, max_val=E - 1)
                sp.dma_start(eraw[:, r, :], wexperts[bass.ds(e, 1)].rearrange("a p n -> p (a n)")).then_inc(ew_in[r], 16)

            def load_shared(u):
                sp.dma_start(sraw[:, u % 2 * WCOLS:(u % 2 + 1) * WCOLS], wshared[u]).then_inc(sw_in[u % 2], 16)

            def store_bits(c):
                t = slice(c * CH, (c + 1) * CH)
                sp.wait_ge(bits_ok, (c + 1) * 2 * DC)
                for m, d in ((0, q_dram), (1, k_dram)):
                    sp.dma_start(d.rearrange("(c p) n -> p c n", p=P)[:, :, t], bits[m][:, :, :]).then_inc(bits_out, 16)

            def store_values(c):
                sp.wait_ge(v_read, (c + 1) * TPC)
                sp.wait_ge(ones_ok, 1)
                sp.dma_start(v_dram.rearrange("h p t v -> p h t v")[:, :, c * TPC:(c + 1) * TPC],
                             vals[:, :, :, :]).then_inc(v_out, 16)

            for t in range(NT):
                sp.wait_ge(xT_ok, t + 1)
                sp.dma_start(xT_dram[t], xnT[:, :, 1 + t * P:1 + (t + 1) * P]).then_inc(xT_out, 16)
            for c in range(NCH - 1):
                store_bits(c)
                store_values(c)
            sp.wait_ge(xT_out, 16 * NT)
            sp.wait_ge(eidrow_ok, 1)
            sp.wait_ge(route_read, 1)
            for m in range(3):
                sp.wait_ge(mixed[m], NCH)
            for s in range(4):
                load_expert(s, s)
            for u in range(2):
                load_shared(u)
            sp.dma_start(xtile[:, :, :], xT_dram[0]).then_inc(xtile_in, 16)
            store_bits(NCH - 1)
            sp.wait_ge(proj_ps, NCH * 3 * DC)
            sp.dma_start(xt[:, :], x[0:P, :]).then_inc(xt_in, 16)

            def load_head(m, hh):
                h = m * 2 + hh
                for dst, d in ((queries, q_dram), (keys, k_dram)):
                    sp.dma_start(dst[:, hh, :], d.rearrange("(h r) n -> h r n", r=DH)[bass.ds(h, 1)].rearrange(
                        "a r n -> r (a n)")).then_inc(head_in[hh], 16)
                sp.dma_start(vraw[:, hh].rearrange("p t v -> p (t v)"), v_dram[bass.ds(h, 1)].rearrange(
                    "a p t v -> p (a t v)")).then_inc(head_in[hh], 16)

            def step(base, f, i):
                s = base + f
                if isinstance(s, int) and s + 2 < NS:
                    sp.wait_ge(sw_low, s + 1)
                    load_shared(s + 2)
                if isinstance(s, int) and s == 1:
                    store_values(NCH - 1)
                if f == 0:
                    return
                if isinstance(s, int) and s == SLOTS - 1:
                    sp.wait_ge(edn_low, SLOTS)
                    sp.wait_ge(eup_low, SLOTS)
                    sp.wait_ge(bits_out, 16 * 2 * NCH)
                    sp.wait_ge(v_out, 16 * NCH)
                    load_head(0, 0)
                    load_head(0, 1)
                sp.wait_ge(y_ok, s)
                sp.dma_start(y_slots[bass.ds(s - 1, 1)].rearrange("a p d -> p (a d)"), ysb[:, (f - 1) % 2, :]).then_inc(
                    y_out[(f - 1) % 2], 16)
                if not isinstance(s, int) or s + 3 < SLOTS:
                    sp.wait_ge(edn_low, s)
                    load_expert(s + 3, (f + 3) % 4)
                if f == 2 and not (isinstance(i, int) and i == NT - 1):
                    sp.wait_ge(st_low, i + 1)
                    sp.dma_start(xtile[:, :, :], xT_dram[bass.ds(i + 1, 1)].rearrange("a p c n -> p (a c) n")).then_inc(xtile_in, 16)
                if f == NS:
                    sp.wait_ge(part_ok, i + 1)
                    sp.dma_start(part_dram[bass.ds(i, 1)].rearrange("a p d -> p (a d)"), psh[:, :]).then_inc(part_out, 16)
                    sp.dma_start(xt[:, :], x[bass.ds((i + 1) * P, P), :]).then_inc(xt_in, 16)

            slot_steps(step, lambda n: sp.Fori(1, 1 + n))
            sp.wait_ge(y_ok, SLOTS)
            sp.dma_start(y_slots[SLOTS - 1], ysb[:, (SLOTS - 1) % 2, :]).then_inc(y_out[(SLOTS - 1) % 2], 16)
            sp.wait_ge(part_ok, NT)
            sp.dma_start(part_dram[NT - 1], psh[:, :]).then_inc(part_out, 16)

            sp.wait_ge(part_out, 16 * NT)
            sp.wait_ge(y_out[0], 16 * SLOTS // 2)
            sp.wait_ge(y_out[1], 16 * SLOTS // 2)
            sp.wait_ge(sh_ps, SLOTS)
            for c in chunks:
                sp.dma_start(acc[:, c * TPC:(c + 1) * TPC, :],
                             part_dram[c * TPC:(c + 1) * TPC].rearrange("t p d -> p t d")).then_inc(acc_in[c], 16)
            with sp.Fori(0, H // 2 - 1) as m:
                for hh in range(2):
                    sp.wait_ge(pv_ps, m * NP + (last_of(NCH * hh + NCH - 1) + PROBS_FREE))
                    load_head(m + 1, hh)
            ov = out.rearrange("(t p) d -> p t d", p=P)
            for heads, units_done in ((slice(0, (H - 1) * DH), H // 2 * NU - 2 * NCH), (slice((H - 1) * DH, D), H // 2 * NU - NCH)):
                for n, c in enumerate(chunks):
                    tiles = slice(c * TPC, (c + 1) * TPC)
                    sp.wait_ge(rows_added, (n + 1) * TPC + ROWS_FREE)
                    sp.wait_ge(unit_ok, units_done + n + 1)
                    sp.dma_start(ov[:, tiles, heads], acc[:, tiles, heads]).then_inc(fin_out, 16)
            sp.wait_ge(fin_out, 16 * 2 * NCH)

        @block.gpsimd
        def _(pool):
            own = Own(pool, pool_own)
            own.mark(pool.memset(ident[:, :], 0.0))
            own.mark(pool.memset(ones_b[:, :], 1.0))
            own.mark(pool.memset(before[:, :], 1.0))
            own.mark(pool.memset(mhalf[:, :], -0.5))
            own.mark(pool.memset(xnT[:, :, 0:1], 0.0))
            own.mark(pool.memset(ones_e[:, :], 1.0))
            own.mark(pool.iota(iota_e[:, :], [[1, E]], base=0, channel_multiplier=0, allow_small_or_imprecise_dtypes=True))
            own.mark(pool.iota(iota_s[:, :], [[1, P]], base=0, channel_multiplier=0, allow_small_or_imprecise_dtypes=True))
            own.mark(pool.iota(tok_i[:, :], [[P, NT]], base=0, channel_multiplier=1, allow_small_or_imprecise_dtypes=True))
            own.step(pool.iota(part_i[:, :], [[0, 1]], base=0, channel_multiplier=1, allow_small_or_imprecise_dtypes=True))
            own.step(pool.affine_select(out=ident[:, :], in_=ident[:, :], compare_op=ALU.not_equal, fill=1.0, base=0,
                                        pattern=[[-1, P]], channel_multiplier=1))
            own.step(pool.affine_select(out=before[:, :], in_=before[:, :], compare_op=ALU.is_gt, fill=0.0, base=0,
                                        pattern=[[1, P]], channel_multiplier=-1))
            pool.tensor_scalar(masked_b[:, :], ident[:, :], MASKED, None, ALU.mult).then_inc(consts, 1)

            def differences(c):
                pool.wait_ge(xT_ok, (c + 1) * TPC)
                for m in range(2):
                    at_least(pool, mixed[m], c)
                pool.tensor_tensor(shift, xnT[:, :, c * CH:c * CH + CH], xnT[:, :, c * CH + 1:c * CH + CH + 1],
                                   ALU.subtract).then_inc(shift_ok, 1)

            def weights_low(m):
                pool.wait_ge(w_high[m], 1)
                pool.tensor_tensor(w_r[m][:, 1], w_raw[m][:, :, :], as_f32(w_r[m][:, 0]), ALU.subtract).then_inc(w_low[m], 1)

            def input_low(g):
                pool.wait_ge(mix_high, g + 1)
                pool.tensor_tensor(mix_r[g % 2][:, 1], mraw[g % 2][:, :, :], as_f32(mix_r[g % 2][:, 0]),
                                   ALU.subtract).then_inc(mix_low, 1)

            def values_input(c):
                g = 3 * c + 2
                pool.wait_ge(shift_ok, c + 1)
                pool.wait_ge(mix_low, g - 1)
                own.step(pool.tensor_tensor(mraw[g % 2][:, :, :], shift, cols_sb[:, COL_XV:COL_XV + DC].unsqueeze(2).to_broadcast([P, DC, CH]),
                                            ALU.mult))
                pool.tensor_tensor(mraw[g % 2][:, :, :], mraw[g % 2][:, :, :], xnT[:, :, c * CH + 1:c * CH + CH + 1],
                                   ALU.add).then_inc(mixed[2], 1)

            for g in range(NCH):
                if g == NCH - 1:
                    differences(0)
                pool.wait_ge(var_eps, g + 1)
                t = slice(g * TPC, (g + 1) * TPC)
                pool.tensor_tensor(rstd[:, t], mv[:, t, 1], mhalf[:, :], ALU.pow).then_inc(rstd_ok, 1)

            weights_low(0)
            pool.wait_ge(cols_in, 16)
            for c in range(NCH):
                input_low(3 * c)
                if c == 0:
                    weights_low(1)
                    input_low(1)
                    values_input(0)
                    pool.wait_ge(h1_ps, 1)
                    pool.memset(vals[:, :, :, :].rearrange("p h t v -> p (h t) v")[:, :, DH:VW], 1.0).then_inc(ones_ok, 1)
                    pool.wait_ge(rows_in, 16)
                    pool.tensor_tensor(rows_sb[:, ROW_E1:ROW_E1 + D], rows_sb[:, ROW_E1:ROW_E1 + D],
                                       rows_sb[:, ROW_E0:ROW_E0 + D], ALU.subtract).then_inc(scale_ok, 1)
                else:
                    values_input(c)
                    input_low(3 * c + 1)
                if c + 1 < NCH:
                    differences(c + 1)
                input_low(3 * c + 2)

            def gather(s, r):
                own.step(pool.tensor_copy(idx_now[:, r:r + 1], idx[:, bass.ds(s, 1)]))
                pool.nop(nofuse=True)
                pool.indirect_dma_start(out=xg[:, r, :], out_offset=None, in_=xn_dram,
                                        in_offset=bass.IndirectOffsetOnAxis(ap=idx_now[:, r:r + 1], axis=0)).then_inc(
                    xg_in[r], 16)

            pool.wait_ge(xn_out, 16 * NCH)
            pool.wait_ge(idx_ok, 1)
            pool.wait_ge(route_read, 1)
            for s in range(4):
                gather(s, s)

            def step(base, f, i):
                s = base + f
                if f and (not isinstance(s, int) or s + 3 < SLOTS):
                    pool.wait_ge(gt_ps, s)
                    gather(s + 3, (f + 3) % 4)

            slot_steps(step, lambda n: own.loop(n, NS, 1))

            def scale_values(m, hh):
                pool.wait_ge(head_in[hh], m * 48 + 48)
                v = vraw[:, hh, :, 0:DH]
                pool.tensor_tensor(v, v, rows_sb[:, bass.ds(m * (2 * DH) + (ROW_E1 + hh * DH), DH)].unsqueeze(1).to_broadcast([P, NT, DH]),
                                   ALU.mult).then_inc(v_scaled[hh], 1)

            pool.wait_ge(scale_ok, 1)
            scale_values(0, 0)
            pool.wait_ge(y_out[0], 16 * SLOTS // 2)
            pool.wait_ge(y_out[1], 16 * SLOTS // 2)
            pool.wait_ge(part_out, 16 * NT)
            pool.wait_ge(sh_ps, SLOTS)

            pool.nop(nofuse=True).then_inc(combined, 1)
            def experts_sums(m, more):
                for q in range(TPC):
                    if q == 1:
                        scale_values(m, 1)
                    if q == 3 and more:
                        scale_values(m + 1, 0)
                    tile = m * -TPC + (NT - TPC + q)
                    own.step(pool.tensor_copy(idx_now[:, 0:K], sloti[:, bass.ds(tile, 1), :].rearrange("p t k -> p (t k)")))
                    pool.wait_ge(combined, m * TPC + (q + 1))
                    pool.nop(nofuse=True)
                    for k in range(K):
                        pool.indirect_dma_start(
                            out=yrows[:, k, :], out_offset=None, in_=y_dram,
                            in_offset=bass.IndirectOffsetOnAxis(ap=idx_now[:, k:k + 1], axis=0)).then_inc(yrows_in, 16)
                    pool.wait_ge(yrows_in, m * (16 * K * TPC) + 16 * K * (q + 1))
                    pool.wait_ge(rows_added, m * TPC + (q + 1))
                    w = wgt[:, :, bass.ds(tile, 1)].to_broadcast([P, K, D])
                    own.step(pool.tensor_tensor(yrows[:, :, :], yrows[:, :, :], w, ALU.mult))
                    own.step(pool.tensor_tensor(yrows[:, 0:2, :], yrows[:, 0:2, :], yrows[:, 2:4, :], ALU.add))
                    pool.tensor_tensor(ysum[:, q % 2], yrows[:, 0, :], yrows[:, 1, :], ALU.add).then_inc(combined, 1)

            with own.loop(H // 2 - 1, TPC * 3) as m:
                experts_sums(m, True)
            experts_sums(H // 2 - 1, False)

        @block.scalar
        def _(act):
            own = Own(act, act_own)
            def input_high(g):
                act.wait_ge(mixed[g % 3], g // 3 + 1)
                at_least(act, proj_ps, (g - 1) * DC)
                act.activation(mix_r[g % 2][:, 0], mraw[g % 2][:, :, :], ACT.Copy).then_inc(mix_high, 1)

            def weights_high(m, d):
                act.wait_ge(w_in[m], 16)
                return act.activation(w_r[m][:, 0, d], w_raw[m][:, d], ACT.Copy)

            for t in range(NT):
                act.wait_ge(xT_ps, t + 1)
                act.activation(xnT[:, :, 1 + t * P:1 + (t + 1) * P], psum[:, t % 2, :].rearrange("p (c n) -> p c n", c=DC),
                               ACT.Copy).then_inc(xT_ok, 1)
                if TPC <= t < 3 * TPC:
                    m, d = divmod(t - TPC, DC)
                    ins = weights_high(m, d)
                    if d == DC - 1:
                        ins.then_inc(w_high[m], 1)
                if t == NT - 3:
                    input_high(0)

            def values(c, tiles=range(TPC)):
                for t in tiles:
                    u = c * 3 * DC + 2 * DC + t
                    act.wait_ge(proj_ps, u + 1)
                    at_least(act, v_out, 16 * c)
                    act.activation(vals[:, :, t, 0:DH],
                                   psum[:, u % 4, :].rearrange("p (h v) -> p h v", h=H), ACT.Sigmoid).then_inc(v_read, 1)

            def projected(c, m):
                for n in range(DC):
                    j, u = (c * 2 + m) * DC + n, (c * 3 + m) * DC + n
                    act.wait_ge(proj_ps, u + 1)
                    at_least(act, bits_read, j - 1)
                    act.activation(qk[:, j % 2], psum[:, u % 4, :], ACT.Copy).then_inc(qk_read, 1)

            input_high(1)
            for d in range(DC):
                ins = weights_high(2, d)
            ins.then_inc(w_high[2], 1)
            projected(0, 0)
            input_high(2)
            act.wait_ge(h1_ps, 1)
            act.wait_ge(cols_in, 16)
            for j in range(2):
                g = act.activation(h1[:, j:j + 1], psum[:, 6, j:j + 1], ACT.Gelu, bias=cols_sb[:, COL_B1 + j:COL_B1 + j + 1],
                                   scale=1.0 / N)
            g.then_inc(h1_ok, 1)
            projected(0, 1)
            input_high(3)
            values(0, [0, 1])
            act.wait_ge(z_ok, 1)
            act.activation(td[:, 4:8], td[:, 0:4], ACT.Exp, bias=td[:, 8:9], accum_out=td[:, 9:10]).then_inc(z_exp, 1)
            values(0, [2, 3])
            input_high(4)
            act.wait_ge(lg_shift, 1)
            act.activation(ex, ex, ACT.Exp).then_inc(lg_exp, 1)
            for c in range(1, NCH - 1):
                projected(c, 0)
                input_high(3 * c + 2)
                projected(c, 1)
                input_high(3 * c + 3)
                values(c)
                input_high(3 * c + 4)
            projected(NCH - 1, 0)
            input_high(3 * NCH - 1)
            projected(NCH - 1, 1)

            def expert_high(s, f, cols, done, used):
                act.wait_ge(ew_in[f % 4], 16 * (s // 4 + 1) if isinstance(s, int) else (s - f % 4) * 4 + 16)
                at_least(act, used, s - 1)
                act.activation(ew_r[f % 2][:, 0, cols], eraw[:, f % 4, cols], ACT.Copy).then_inc(done, 1)

            def shared_high(u):
                act.wait_ge(sw_in[u % 2], 16 * (u // 2 + 1))
                if u == NS - 1:
                    act.wait_ge(bits_out, 16 * 2 * NCH)
                    act.wait_ge(v_out, 16 * NCH)
                act.activation(sw_r[:, u, 0], sraw[:, u % 2 * WCOLS:(u % 2 + 1) * WCOLS], ACT.Copy).then_inc(sw_high, 1)

            def tokens_high(s, f):
                act.wait_ge(gt_ps, s + 1)
                at_least(act, gu_ps[0], s - 1)
                act.activation(xT_r[:, f % 2, 0], psum[:, 0, :].rearrange("p (c n) -> p c n", c=DC), ACT.Copy).then_inc(x_high, 1)

            def tile_high(i):
                act.wait_ge(xtile_in, i * 16 + 16)
                at_least(act, gu_ps[1], i * NS)
                act.activation(xst_r[:, 0], xtile[:, :, :], ACT.Copy).then_inc(st_high, 1)

            def silu(kind, s):
                act.wait_ge(gu_ps[kind], s + 1)
                at_least(act, h_ok[kind], s)
                act.activation(sg[:, kind], psum[:, 1 + kind, 0:F], ACT.Silu).then_inc(silu_ok[kind], 1)

            def hidden_high(kind, s):
                act.wait_ge(hT_ps[kind], s + 1)
                at_least(act, y_ps if kind == 0 else sh_ps, s)
                act.activation(h_r[:, kind, 0], psum[:, 3 + kind, 0:P], ACT.Copy).then_inc(hT_high[kind], 1)

            def rows_out(y, f):
                act.wait_ge(y_ps, y + 1)
                at_least(act, y_out[f % 2], 16 * (y // 2) if isinstance(y, int) else (y - f % 2) * 8)
                act.activation(ysb[:, f % 2], psum[:, 5 + f % 2, :], ACT.Copy).then_inc(y_ok, 1)

            act.wait_ge(bits_ok, NCH * 2 * DC)
            act.wait_ge(idx_ok, 1)
            for m in range(3):
                act.wait_ge(mixed[m], NCH)
            expert_high(0, 0, UP, eup_exp, gu_ps[0])
            expert_high(0, 0, DOWN, edn_high, y_ps)
            values(NCH - 1)
            act.wait_ge(proj_ps, NCH * 3 * DC)
            tile_high(0)
            shared_high(0)
            tokens_high(0, 0)

            def step(base, f, i):
                s = base + f
                more = not isinstance(s, int) or s + 1 < SLOTS
                if more:
                    expert_high(s + 1, f + 1, UP, eup_exp, gu_ps[0])
                silu(0, s)
                if f:
                    hidden_high(1, s - 1)
                if more:
                    tokens_high(s + 1, f + 1)
                if f:
                    rows_out(s - 1, f - 1)
                if more:
                    expert_high(s + 1, f + 1, DOWN, edn_high, y_ps)
                if isinstance(s, int) and s + 1 < NS:
                    shared_high(s + 1)
                silu(1, s)
                hidden_high(0, s)
                if f == NS - 1 and more:
                    tile_high(i + 1)

            slot_steps(step, lambda n: act.Fori(1, 1 + n))
            act.activation(td[:, 0:1], td[:, 9:10], ACT.Exp)
            hidden_high(1, SLOTS - 1)
            rows_out(SLOTS - 1, SLOTS - 1)

            act.wait_ge(edn_low, SLOTS)
            act.wait_ge(eup_low, SLOTS)
            act.wait_ge(gt_ps, SLOTS)
            act.wait_ge(y_ps, SLOTS)
            act.wait_ge(gu_ps[0], SLOTS)
            act.wait_ge(gu_ps[1], SLOTS)
            act.wait_ge(x_low, SLOTS)

            def values_high(m, hh):
                act.wait_ge(v_scaled[hh], m + 1)
                act.activation(v_r[hh][:, 0], vraw[:, hh], ACT.Copy).then_inc(v_high[hh], 1)

            act.nop(nofuse=True).then_inc(p_exp, SCORES_FREE)
            act.nop(nofuse=True).then_inc(oT_ok, SUMS_FREE)

            def sums_out(m, v):
                act.wait_ge(pv_ps, m * NP + (last_of(v) + PROBS_FREE))
                act.wait_ge(o_ps, m * NU + (v + 1))
                act.activation(osb[:, v % 2], psum[0:VW, 4 + v % 2, :], ACT.Copy).then_inc(oT_ok, 1)

            def part(m, a, b, old):
                for n in range(a, b):
                    v, p = pairs[n]
                    o = first_column(units[v][1], p)
                    act.wait_ge(s_ps, m * NP + (n + 1))
                    act.wait_ge(pv_ps, m * NP + (n + 1))
                    scores = psum[:, 2 * (n % 2):2 * (n % 2) + 2, o:CH]
                    ins = act.activation(pf[:, n % 4, :, o:CH], scores, ACT.Exp, scale=4.0)
                    if not low_and_high(n):
                        ins = act.activation(ph[:, n % 4, :, o:CH], scores, ACT.Exp, scale=4.0)
                    ins.then_inc(p_exp, 1)
                    if n == 0 and isinstance(m, int):
                        values_high(0, 0)
                    if n == LEAD - 1:
                        if isinstance(m, int):
                            act.wait_ge(y_out[0], 16 * SLOTS // 2)
                            act.wait_ge(y_out[1], 16 * SLOTS // 2)
                            act.wait_ge(part_out, 16 * NT)
                            act.wait_ge(sh_ps, SLOTS)
                    if n == VALUES_STEPS[1]:
                        values_high(m, 1)
                    if n == VALUES_STEPS[0] and not isinstance(m, int):
                        values_high(m + 1, 0)
                    for w in range(NU):
                        if later(SUMS, w) == (n, False):
                            sums_out(m, w)
                        if later(SUMS, w) == (n, True) and old is not None:
                            sums_out(old, w)

            rounds(part, lambda trips: act.Fori(0, trips))
            for w in range(NU):
                if later(SUMS, w)[1]:
                    sums_out(H // 2 - 1, w)

        @block.tensor
        def _(pe):
            pe.wait_ge(consts, 1)
            for t in range(NT + 2):
                if t < NT:
                    pe.wait_ge(xn_ok, t + 1)
                    at_least(pe, xT_ok, t - 1)
                    for d in range(DC):
                        mm = pe.transpose(psum[:, t % 2, d * P:(d + 1) * P], xs[:, t, d * P:(d + 1) * P], ident[:, :])
                    mm.then_inc(xT_ps, 1)
                if t >= 2:
                    b = t - 2
                    pe.wait_ge(wr_in, 16)
                    pe.wait_ge(xT_ok, b + 1)
                    for d in range(DC):
                        mm = pe.matmul(psum[:, 4 + b // 8, (b % 8) * E:(b % 8 + 1) * E], xnT[:, d, 1 + b * P:1 + (b + 1) * P],
                                       wr_sb[:, d, :], start=d == 0, stop=d == DC - 1)
            mm.then_inc(lg_ps, 1)

            def in_parts(dst, lhs, rhs, first, last):
                for n, (a, b) in enumerate(((1, 0), (0, 1), (0, 0))):
                    mm = pe.matmul(dst, lhs[a], rhs[b], start=first and n == 0, stop=last and n == 2)
                return mm

            def project(c, m, after=lambda n: None):
                g = 3 * c + m
                pe.wait_ge(w_low[m], 1)
                pe.wait_ge(mix_low, g + 1)
                for n in range(DC):
                    u = g * DC + n
                    if u >= 4:
                        v = u - 4
                        vc, vr = v // (3 * DC), v % (3 * DC)
                        if vr < 2 * DC:
                            pe.wait_ge(qk_read, vc * 2 * DC + vr + 1)
                        else:
                            pe.wait_ge(v_read, vc * TPC + vr - 2 * DC + 1)
                    for d in range(DC):
                        w, x = [w_r[m][:, a, d, :] for a in range(2)], [mix_r[g % 2][:, a, d, :] for a in range(2)]
                        part = slice(n * P, (n + 1) * P)
                        lhs, rhs = ([a[:, part] for a in w], x) if m < 2 else ([a[:, part] for a in x], w)
                        mm = in_parts(psum[:, u % 4, :], lhs, rhs, d == 0, d == DC - 1)
                    mm.then_inc(proj_ps, 1)
                    after(n)

            project(0, 0)
            pe.wait_ge(te_in, 16)
            pe.wait_ge(xm_ok, 1)
            for j in range(2):
                for d in range(DC):
                    mm = pe.matmul(psum[:, 6, j:j + 1], te1_sb[:, d, j * P:(j + 1) * P], xm[:, 0, d:d + 1],
                                   start=d == 0, stop=d == DC - 1)
            mm.then_inc(h1_ps, 1)
            project(0, 1)
            pe.wait_ge(h1b_ok, 1)
            pe.wait_ge(te2_in, 16)
            for j in range(2):
                mm = pe.matmul(psum[:, 7, 0:ND], h1b[:, j, :], te2_sb[:, j, :], start=j == 0, stop=j == 1)
            mm.then_inc(z_ps, 1)
            project(0, 2)
            project(1, 0)
            project(1, 1)
            pe.wait_ge(onehot_ok, 1)
            for m, w in ((0, before), (1, ones_b)):
                for b in range(2):
                    for k in range(K):
                        mm = pe.matmul(psum[:, 4 + 2 * m + b, :], w[:, :], oh[:, k, b * 8:(b + 1) * 8, :].rearrange("p t e -> p (t e)"),
                                       start=k == 0, stop=k == K - 1)
                mm.then_inc(count_ps if m else rank_ps, 1)
            project(1, 2)
            for m in range(3):
                project(2, m)
            pe.wait_ge(eid_ok, 1)
            pe.matmul(psum[0:1, 6, 0:P], eid[:, :], ident[:, :], start=True, stop=True).then_inc(eid_ps, 1)

            def listed(m, n):
                for j in list_share(m, n):
                    pe.wait_ge(pair_ok, j + 1)
                    pe.matmul(psum[:, 4, 0:P], list_a[:, j % 8, :], list_b[:, j % 8, :], start=j == 0,
                              stop=j == K * NT - 1).then_inc(list_ps, 1)

            for m in range(3):
                project(3, m, lambda n: listed(m, n))

            def transpose_tokens(s, f):
                pe.wait_ge(xg_in[f % 4], 16 * (s // 4 + 1) if isinstance(s, int) else (s - f % 4) * 4 + 16)
                at_least(pe, x_low, s)
                for d in range(DC):
                    mm = pe.transpose(psum[:, 0, d * P:(d + 1) * P], xg[:, f % 4, d * P:(d + 1) * P], ident[:, :])
                mm.then_inc(gt_ps, 1)

            def up(kind, s, lhs, w):
                at_least(pe, h_ok[kind], s)
                for d in range(DC):
                    mm = in_parts(psum[:, 1 + kind, 0:2 * F], [lhs[:, a, d, :] for a in range(2)],
                                  [gate_up(w[:, b], d) for b in range(2)], d == 0, d == DC - 1)
                mm.then_inc(gu_ps[kind], 1)

            def transpose_hidden(kind, s):
                pe.wait_ge(h_ok[kind], s + 1)
                at_least(pe, hT_low[kind], s)
                pe.transpose(psum[:, 3 + kind, 0:P], hb[:, kind, :], ident[:, :]).then_inc(hT_ps[kind], 1)

            def down_expert(y, f):
                pe.wait_ge(edn_low, y + 1)
                pe.wait_ge(hT_low[0], y + 1)
                at_least(pe, y_ok, y - 1)
                w = ew_r[f % 2]
                in_parts(psum[:, 5 + f % 2, :], [h_r[:, 0, a, :] for a in range(2)], [down(w[:, b]) for b in range(2)],
                         True, True).then_inc(y_ps, 1)

            def down_shared(y, f, tile):
                pe.wait_ge(hT_low[1], y + 1)
                u = f % NS
                if u == 0:
                    at_least(pe, sh_read, tile)
                in_parts(psum[:, 7, :], [h_r[:, 1, a, :] for a in range(2)], [down(sw_r[:, u, b]) for b in range(2)],
                         u == 0, u == NS - 1).then_inc(sh_ps, 1)

            pe.wait_ge(idx_ok, 1)
            pe.wait_ge(eidrow_ok, 1)
            pe.wait_ge(qk_read, NCH * 2 * DC)
            pe.wait_ge(v_read, NT)
            transpose_tokens(0, 0)

            def step(base, f, i):
                s = base + f
                pe.wait_ge(x_low, s + 1)
                pe.wait_ge(eup_low, s + 1)
                up(0, s, xT_r[:, f % 2], ew_r[f % 2])
                if f:
                    down_expert(s - 1, f - 1)
                    transpose_hidden(1, s - 1)
                u = f % NS
                tile = i if f < NS else i + 1
                if not isinstance(s, int) or s + 1 < SLOTS:
                    transpose_tokens(s + 1, f + 1)
                if u == 0:
                    pe.wait_ge(st_low, tile + 1)
                if isinstance(s, int) and s < NS:
                    pe.wait_ge(sw_low, s + 1)
                up(1, s, xst_r, sw_r[:, u])
                if f:
                    down_shared(s - 1, f - 1, i)
                transpose_hidden(0, s)

            slot_steps(step, lambda n: pe.Fori(1, 1 + n))
            down_expert(SLOTS - 1, SLOTS - 1)
            transpose_hidden(1, SLOTS - 1)
            down_shared(SLOTS - 1, SLOTS - 1, NT - 1)

            pe.wait_ge(x_low, SLOTS)
            pe.wait_ge(h_ok[0], SLOTS)
            pe.wait_ge(h_ok[1], SLOTS)
            pe.wait_ge(hT_low[0], SLOTS)
            pe.wait_ge(hT_low[1], SLOTS)
            pe.wait_ge(y_ok, SLOTS)
            pe.wait_ge(sh_read, NT)
            pe.nop(nofuse=True).then_inc(pv_ps, PROBS_FREE)

            def scores(m, n):
                v, p = pairs[n]
                hh, c = units[v]
                o = first_column(c, p)
                if n == first_pair[v] and v % NCH == 0:
                    pe.wait_ge(head_in[hh], m * 48 + 48)
                pe.wait_ge(p_exp, m * NP + (n + 1))
                for j in range(2):
                    bank = psum[:, 2 * (n % 2) + j, :]
                    d = 2 * p + j - TPC * c
                    mm = pe.matmul(bank[:, o:CH], keys[:, hh, (2 * p + j) * P:(2 * p + j + 1) * P],
                                   queries[:, hh, c * CH + o:(c + 1) * CH], start=True, stop=d < 0)
                    if d >= 0:
                        mm = pe.matmul(bank[:, d * P:(d + 1) * P], before[:, :], masked_b[:, :], start=False, stop=True)
                mm.then_inc(s_ps, 1)

            def weighted(m, n):
                v, p = pairs[n]
                hh, c = units[v]
                if p == 0 and v % NCH == 0:
                    pe.wait_ge(v_low[hh], m + 1)
                pe.wait_ge(p_low, m * NP + (n + 1))
                if p == 0:
                    pe.wait_ge(oT_ok, m * NU + (v + 1))
                for j in range(2):
                    o = max(2 * p + j - TPC * c, 0) * P
                    mm = in_parts(psum[0:VW, 4 + v % 2, o:CH], [v_r[hh][:, a, 2 * p + j, :] for a in range(2)],
                                  [b[:, n % 4, j, o:CH] for b in (ph, pl)], 2 * p + j == 0, 2 * p + j == TPC * (c + 1) - 1)
                mm.then_inc(pv_ps, 1)

            def back(m, v):
                pe.wait_ge(oT_ok, m * NU + (v + 1 + SUMS_FREE))
                pe.wait_ge(o_read, m * NU + (v + 1))
                for t in range(TPC):
                    mm = pe.transpose(psum[:, 6 + v % 2, t * VW:(t + 1) * VW], osb[:, v % 2, t * P:(t + 1) * P], ident[0:VW, 0:VW])
                mm.then_inc(o_ps, 1)

            def part(m, a, b, old):
                for n in range(a, b):
                    if n + AHEAD < NP:
                        scores(m, n + AHEAD)
                    elif not (isinstance(m, int) and m == H // 2 - 1):
                        scores(m + 1, n + AHEAD - NP)
                    weighted(m, n)
                    for v in range(NU):
                        if later(BACK, v) == (n, False):
                            back(m, v)
                        if later(BACK, v) == (n, True) and old is not None:
                            back(old, v)

            for n in range(AHEAD):
                scores(0, n)
            rounds(part, lambda trips: pe.Fori(0, trips))
            for v in range(NU):
                if later(BACK, v)[1]:
                    back(H // 2 - 1, v)

        @block.vector
        def _(dve):
            own = Own(dve, dve_own)

            for g in range(NCH):
                dve.wait_ge(x_in[g], 16)
                for t in range(g * TPC, (g + 1) * TPC):
                    own.mark(dve.bn_stats(stats[:, t, :], xs[:, t, :]))
                own.wait()
                for t in range(g * TPC, (g + 1) * TPC):
                    own.mark(dve.bn_aggr(mv[:, t, :], stats[:, t, :]))
                own.wait()
                v = mv[:, g * TPC:(g + 1) * TPC, 1]
                dve.tensor_scalar(v, v, EPS, None, ALU.add).then_inc(var_eps, 1)
                if g:
                    normalise(dve, g - 1, rstd_ok, xn_ok, xs, mv, rstd)
            normalise(dve, NCH - 1, rstd_ok, xn_ok, xs, mv, rstd)
            def shift_mix(m, c):
                g = 3 * c + m
                dve.wait_ge(shift_ok, c + 1)
                at_least(dve, mix_low, g - 1)
                if g == 1:
                    dve.wait_ge(w_low[0], 1)
                for d in range(DC):
                    ins = dve.scalar_tensor_tensor(mraw[g % 2][:, d], shift[:, d], cols_sb[:, m * DC + d:m * DC + d + 1],
                                                   xnT[:, d, c * CH + 1:(c + 1) * CH + 1], ALU.mult, ALU.add)
                ins.then_inc(mixed[m], 1)

            def trigger(m, c, after=lambda n: None):
                for n in range(DC):
                    j = (c * 2 + m) * DC + n
                    dve.wait_ge(qk_read, j + 1)
                    own.mark(dve.tensor_scalar(low, qk[:, j % 2], THRESHOLD, 0.5, ALU.is_gt, ALU.subtract))
                    dve.tensor_scalar(high, qk[:, j % 2], -THRESHOLD, 0.5, ALU.is_ge, ALU.subtract).then_inc(bits_read, 1)
                    dve.wait_ge(bits_read, j + 1)
                    own.wait()
                    at_least(dve, bits_out, 16 * 2 * c)
                    dve.tensor_tensor_scan(bits[m][:, n, :], high, low, bits[m][:, n, CH - 1:CH] if c else -0.5,
                                           ALU.min, ALU.max).then_inc(bits_ok, 1)
                    dve.wait_ge(bits_ok, j + 1)
                    after(n)

            dve.wait_ge(cols_in, 16)
            shift_mix(0, 0)
            shift_mix(1, 0)
            for g in range(NCH):
                dve.wait_ge(xT_ok, (g + 1) * TPC)
                own.mark(dve.tensor_reduce(xm[:, g, :], xnT[:, :, 1 + g * CH:1 + (g + 1) * CH], AX_X, ALU.add))
            own.wait()
            own.step(dve.tensor_tensor(xm[:, 0:2, :], xm[:, 0:2, :], xm[:, 2:4, :], ALU.add))
            dve.tensor_tensor(xm[:, 0, :], xm[:, 0, :], xm[:, 1, :], ALU.add).then_inc(xm_ok, 1)
            dve.wait_ge(w_high[2], 1)
            dve.tensor_tensor(w_r[2][:, 1], w_raw[2][:, :, :], as_f32(w_r[2][:, 0]), ALU.subtract).then_inc(w_low[2], 1)
            dve.wait_ge(w_low[2], 1)
            trigger(0, 0)
            dve.wait_ge(h1_ok, 1)
            for j in range(2):
                ins = dve.tensor_copy(h1b[:, j, :], h1[:, j:j + 1].to_broadcast([P, P]))
            ins.then_inc(h1b_ok, 1)
            shift_mix(0, 1)
            trigger(1, 0)
            shift_mix(1, 1)

            dve.wait_ge(z_ps, 1)
            dve.wait_ge(rows_in, 16)
            own.step(dve.tensor_tensor(td[:, 0:4], psum[:, 7, 0:ND], rows_sb[:, ROW_B2:ROW_B2 + ND], ALU.add))
            own.step(dve.tensor_reduce(td[:, 10:11], td[:, 0:4], AX_X, ALU.max))
            dve.tensor_scalar(td[:, 8:9], td[:, 10:11], -1.0, None, ALU.mult).then_inc(z_ok, 1)
            dve.wait_ge(z_exp, 1)
            own.step(dve.reciprocal(td[:, 11:12], td[:, 9:10]))
            own.step(dve.tensor_scalar(td[:, 12:16], td[:, 4:8], td[:, 11:12], 0.5, ALU.mult, ALU.mult))
            aff = rows_sb[:, ROW_AFF:ROW_AFF + ND * E].rearrange("p (n e) -> p n e", n=ND)
            own.step(dve.tensor_scalar(dom[:, :], aff[:, 0], td[:, 12:13], None, ALU.mult))
            for n in range(1, ND):
                own.step(dve.scalar_tensor_tensor(dom[:, :], aff[:, n], td[:, 12 + n:13 + n], dom[:, :], ALU.mult, ALU.add))
            dve.wait_ge(lg_ps, 1)
            dve.wait_ge(xn_out, 16 * NCH)
            dve.wait_ge(xT_ps, NT)
            own.step(dve.tensor_tensor(lg, psum[:, 4:6, :].rearrange("p b (t e) -> p (b t) e", e=E),
                                       dom[:, :].unsqueeze(1).to_broadcast([P, NT, E]), ALU.add))
            own.mark(dve.tensor_tensor(lb, lg, rows_sb[:, ROW_RB:ROW_RB + E].unsqueeze(1).to_broadcast([P, NT, E]), ALU.add))
            own.step(dve.tensor_reduce(mx[:, :], lg, AX_X, ALU.max))
            dve.tensor_tensor(ex, lg, mx[:, :].unsqueeze(2).to_broadcast([P, NT, E]), ALU.subtract).then_inc(lg_shift, 1)
            for t in range(NT):
                own.mark(dve.max(top[:, t, :], lb[:, t, :]))
            own.wait()
            for t in range(NT):
                own.mark(dve.max_index(topi[:, t, :], top[:, t, :], lb[:, t, :]))
            own.wait()
            own.step(dve.tensor_copy(topf[:, :, :], topi[:, :, 0:K]))
            for k in range(K):
                ins = dve.tensor_tensor(oh[:, k], iota_e[:, :].unsqueeze(1).to_broadcast([P, NT, E]),
                                        topf[:, :, k:k + 1].to_broadcast([P, NT, E]), ALU.is_equal)
            ins.then_inc(onehot_ok, 1)
            for m in range(2):
                trigger(m, 1)
                shift_mix(m, 2)

            dve.wait_ge(onehot_ok, 1)
            dve.wait_ge(lg_exp, 1)
            own.step(dve.tensor_reduce(zs[:, :], ex, AX_X, ALU.add))
            own.step(dve.reciprocal(zs[:, :], zs[:, :]))
            for k in range(K):
                own.step(dve.tensor_tensor(prod, oh[:, k], ex, ALU.mult))
                own.step(dve.tensor_reduce(wgt[:, k, :], prod, AX_X, ALU.add))
            own.step(dve.tensor_tensor(wgt[:, :, :], wgt[:, :, :], zs[:, :].unsqueeze(1).to_broadcast([P, K, NT]), ALU.mult))
            own.step(dve.tensor_reduce(wsum[:, :], wgt[:, :, :].rearrange("p k t -> p t k"), AX_X, ALU.add))
            own.step(dve.tensor_scalar(wsum[:, :], wsum[:, :], 1e-8, None, ALU.add))
            own.step(dve.reciprocal(wsum[:, :], wsum[:, :]))
            own.step(dve.tensor_tensor(wgt[:, :, :], wgt[:, :, :], wsum[:, :].unsqueeze(1).to_broadcast([P, K, NT]), ALU.mult))
            def pair(n):
                t, k = n // K, n % K
                at_least(dve, list_ps, n - 7)
                dve.tensor_scalar(list_a[:, n % 8, :], iota_s[:, :], lof[:, k, t:t + 1], None, ALU.is_equal)
                dve.tensor_scalar(list_b[:, n % 8, :], iota_s[:, :], hif[:, k, t:t + 1], tok_i[:, t:t + 1],
                                  ALU.is_equal, ALU.mult).then_inc(pair_ok, 1)

            trigger(0, 2)
            shift_mix(0, 3)
            dve.wait_ge(count_ps, 1)
            counts = psum[:, 6:8, :].rearrange("p b (t e) -> p (b t) e", e=E)
            own.step(dve.tensor_scalar(cum[:, 0, :], counts[:, 0, :], 0.0, None, ALU.mult))
            for t in range(NT - 1):
                own.step(dve.tensor_tensor(cum[:, t + 1, :], counts[:, t, :], cum[:, t, :], ALU.add))
            own.step(dve.tensor_tensor(cnt[:, :], counts[:, NT - 1, :], cum[:, NT - 1, :], ALU.add))
            own.step(dve.tensor_scalar(cnti[:, :], cnt[:, :], float(P - 1), None, ALU.add))
            own.step(dve.tensor_scalar(cnti[:, :], cnti[:, :], 7, None, ALU.arith_shift_right))
            own.step(dve.tensor_copy(cnt[:, :], cnti[:, :]))
            own.step(dve.tensor_tensor_scan(incl[:, :], ones_e[:, :], cnt[:, :], 0.0, ALU.mult, ALU.add))
            own.step(dve.tensor_tensor(cnt[:, :], incl[:, :], cnt[:, :], ALU.subtract))
            own.step(dve.tensor_scalar(cnt[:, :], cnt[:, :], float(P), None, ALU.mult))
            own.step(dve.tensor_scalar(dom[:, :], incl[:, :], part_i[:, :], None, ALU.is_le, ALU.add, accum_out=eid[:, :]))
            dve.tensor_scalar(eid[:, :], eid[:, :], float(E - 1), None, ALU.min).then_inc(eid_ok, 1)
            trigger(1, 2)
            shift_mix(1, 3)

            dve.wait_ge(rank_ps, 1)
            own.step(dve.tensor_tensor(pos, psum[:, 4:6, :].rearrange("p b (t e) -> p (b t) e", e=E), cum, ALU.add))
            own.step(dve.tensor_tensor(pos, pos, cnt[:, :].unsqueeze(1).to_broadcast([P, NT, E]), ALU.add))
            for k in range(K):
                own.step(dve.tensor_tensor(prod, oh[:, k], pos, ALU.mult))
                own.step(dve.tensor_reduce(slotf[:, k, :], prod, AX_X, ALU.add))
            own.mark(dve.tensor_copy(hii[:, :, :], slotf[:, :, :]))
            dve.tensor_copy(sloti[:, :, :], slotf[:, :, :].rearrange("p k t -> p t k")).then_inc(route_read, 1)
            own.wait()
            own.step(dve.tensor_scalar(hii[:, :, :], hii[:, :, :], 7, None, ALU.arith_shift_right))
            own.step(dve.tensor_copy(hif[:, :, :], hii[:, :, :]))
            own.step(dve.scalar_tensor_tensor(lof[:, :, :], hif[:, :, :], -float(P), slotf[:, :, :], ALU.mult, ALU.add))

            dve.wait_ge(eid_ps, 1)
            dve.tensor_copy(eid_row[:, :], psum[0:1, 6, 0:P]).then_inc(eidrow_ok, 1)

            def pairs_of(m, n):
                for j in list_share(m, n):
                    pair(j)

            pairs_of(0, 0)
            for m in range(2):
                trigger(m, 3, lambda n: pairs_of((m * DC + n + 1) // DC, (n + 1) % DC))
            for n in range(1, DC):
                pairs_of(2, n)
            dve.wait_ge(list_ps, K * NT)
            dve.tensor_copy(idx[:, :], psum[:, 4, 0:P]).then_inc(idx_ok, 1)

            def expert_low(s, f, cols, high, done):
                dve.wait_ge(high, s + 1)
                dve.tensor_tensor(ew_r[f % 2][:, 1, cols], eraw[:, f % 4, cols], as_f32(ew_r[f % 2][:, 0, cols]),
                                  ALU.subtract).then_inc(done, 1)

            def shared_low(u):
                dve.wait_ge(sw_high, u + 1)
                dve.tensor_tensor(sw_r[:, u, 1], sraw[:, u % 2 * WCOLS:(u % 2 + 1) * WCOLS], as_f32(sw_r[:, u, 0]),
                                  ALU.subtract).then_inc(sw_low, 1)

            def tokens_low(s, f):
                dve.wait_ge(x_high, s + 1)
                dve.tensor_tensor(xT_r[:, f % 2, 1], psum[:, 0, :].rearrange("p (c n) -> p c n", c=DC),
                                  as_f32(xT_r[:, f % 2, 0]), ALU.subtract).then_inc(x_low, 1)

            def tile_low(i):
                dve.wait_ge(st_high, i + 1)
                dve.tensor_tensor(xst_r[:, 1], xtile[:, :, :], as_f32(xst_r[:, 0]),
                                  ALU.subtract).then_inc(st_low, 1)

            def hidden(kind, s):
                dve.wait_ge(silu_ok[kind], s + 1)
                at_least(dve, hT_ps[kind], s)
                dve.tensor_tensor(hb[:, kind], psum[:, 1 + kind, F:2 * F], sg[:, kind], ALU.mult).then_inc(h_ok[kind], 1)

            def hidden_low(kind, s):
                dve.wait_ge(hT_high[kind], s + 1)
                dve.tensor_tensor(h_r[:, kind, 1], psum[:, 3 + kind, 0:P], as_f32(h_r[:, kind, 0]),
                                  ALU.subtract).then_inc(hT_low[kind], 1)

            def shared_out(i):
                dve.wait_ge(sh_ps, (i + 1) * NS)
                dve.wait_ge(xt_in, 16 * (i + 1))
                at_least(dve, part_out, 16 * i)
                dve.tensor_tensor(psh[:, :], psum[:, 7, :], xt[:, :], ALU.add).then_inc(sh_read, 1)
                dve.wait_ge(sh_read, i + 1)
                dve.tensor_tensor(psh[:, :], psh[:, :], rows_sb[:, ROW_E0:ROW_E0 + D], ALU.add).then_inc(part_ok, 1)

            expert_low(0, 0, UP, eup_exp, eup_low)
            expert_low(0, 0, DOWN, edn_high, edn_low)
            tile_low(0)
            tokens_low(0, 0)
            shared_low(0)

            def step(base, f, i):
                s = base + f
                more = not isinstance(s, int) or s + 1 < SLOTS
                if more:
                    expert_low(s + 1, f + 1, UP, eup_exp, eup_low)
                hidden(0, s)
                if f:
                    hidden_low(1, s - 1)
                if more:
                    tokens_low(s + 1, f + 1)
                    expert_low(s + 1, f + 1, DOWN, edn_high, edn_low)
                hidden(1, s)
                hidden_low(0, s)
                if f == NS:
                    shared_out(i)
                if isinstance(s, int) and s + 1 < NS:
                    shared_low(s + 1)
                if f == NS - 1 and more:
                    tile_low(i + 1)

            slot_steps(step, lambda n: dve.Fori(1, 1 + n))
            hidden_low(1, SLOTS - 1)
            shared_out(NT - 1)

            dve.nop(nofuse=True).then_inc(o_read, SUMS_FREE)
            dve.nop(nofuse=True).then_inc(o_ps, SUMS_FREE)
            dve.nop(nofuse=True).then_inc(rows_added, ROWS_FREE)

            def add_rows(m, q):
                tile = m * -TPC + (NT - TPC + q)
                dve.wait_ge(combined, m * TPC + (q + 2))
                dst = acc[:, bass.ds(tile, 1), :].rearrange("p a d -> p (a d)")
                dve.tensor_tensor(dst, dst, ysum[:, q % 2], ALU.add).then_inc(rows_added, 1)
                dve.wait_ge(rows_added, m * TPC + (q + 1 + ROWS_FREE))

            def values_low(m, hh):
                dve.wait_ge(v_high[hh], m + 1)
                dve.tensor_tensor(v_r[hh][:, 1], vraw[:, hh], as_f32(v_r[hh][:, 0]), ALU.subtract).then_inc(v_low[hh], 1)

            def add(m, v):
                hh, c = units[v]
                dve.wait_ge(o_ps, m * NU + (v + 1 + SUMS_FREE))
                o = psum[:, 6 + v % 2, 0:TPC * VW].rearrange("p (t v) -> p t v", v=VW)
                own.step(dve.reciprocal(rden[:, :], o[:, :, DH]))
                dve.tensor_tensor(xo[:, :, :], o[:, :, 0:DH], rden[:, :].unsqueeze(2).to_broadcast([P, TPC, DH]), ALU.mult).then_inc(o_read, 1)
                dve.wait_ge(o_read, m * NU + (v + 1 + SUMS_FREE))
                dst = acc[:, c * TPC:(c + 1) * TPC, bass.ds(m * (2 * DH) + hh * DH, DH)]
                dve.tensor_tensor(dst, dst, xo[:, :, :], ALU.add).then_inc(unit_ok, 1)
                dve.wait_ge(unit_ok, m * NU + (v + 1))

            def part(m, a, b, old):
                for n in range(a, b):
                    v, p = pairs[n]
                    o = first_column(units[v][1], p)
                    dve.wait_ge(p_exp, m * NP + (n + 1 + SCORES_FREE))
                    if low_and_high(n):
                        own.step(dve.tensor_copy(ph[:, n % 4, :, o:CH], pf[:, n % 4, :, o:CH]))
                    dve.tensor_tensor(pl[:, n % 4, :, o:CH], pf[:, n % 4, :, o:CH], as_f32(ph[:, n % 4, :, o:CH]),
                                      ALU.subtract).then_inc(p_low, 1)
                    if n == 0 and isinstance(m, int):
                        values_low(0, 0)
                    if n == VALUES_STEPS[1]:
                        values_low(m, 1)
                    if n == VALUES_STEPS[0] and not isinstance(m, int):
                        values_low(m + 1, 0)
                    for w in range(NU):
                        if later(ADD, w) == (n, False):
                            add(m, w)
                        if later(ADD, w) == (n, True) and old is not None:
                            add(old, w)
                    if n in ROW_STEPS:
                        add_rows(m, ROW_STEPS.index(n))
                    if n == LEAD - 1 and isinstance(m, int):
                        for c in chunks:
                            dve.wait_ge(acc_in[c], 16)

            rounds(part, lambda trips: own.loop(trips, NU + sum(map(low_and_high, range(NP)))))
            for w in range(NU):
                if later(ADD, w)[1]:
                    add(H // 2 - 1, w)


def normalise(dve, g, rstd_ok, xn_ok, xs, mv, rstd):
    dve.wait_ge(rstd_ok, g + 1)
    for t in range(g * TPC, (g + 1) * TPC):
        dve.tensor_scalar(xs[:, t, :], xs[:, t, :], mv[:, t, 0:1], rstd[:, t:t + 1], ALU.subtract, ALU.mult).then_inc(xn_ok, 1)


def kernel(**inputs):
    import numpy as np
    import concourse.bacc as bacc
    from concourse.bass_utils import run_bass_kernel_spmd

    def get(name):
        return np.asarray(inputs[name])

    def rows_to_partitions(w):
        return w.reshape(DC, P, w.shape[1]).transpose(1, 0, 2)

    def unit_weights(gate, up, down):
        u = gate.shape[0]
        gu = np.stack([gate.reshape(u, DC, P, F), up.reshape(u, DC, P, F)], axis=3)
        gu = gu.transpose(0, 2, 1, 3, 4).reshape(u, P, DC * 2 * F)
        return np.concatenate([gu, down], axis=2)

    def split_shared(w):
        return w.reshape(2, D, NS // 2, F).transpose(0, 2, 1, 3).reshape(NS, D, F)

    def by_partition(v):
        return v.reshape(-1, P).T

    arrays = {
        "x": get("L0_attn_x").reshape(N, D),
        "wqkv": np.stack([rows_to_partitions(get(n).T) for n in ("L0_attn_Wq", "L0_attn_Wk", "L0_attn_Wv")]),
        "cols": np.concatenate([by_partition(get(n)) for n in ("L0_attn_x_q", "L0_attn_x_k", "L0_attn_x_v", "L0_ffn_te_b1")], axis=1),
        "rows": np.concatenate([get("L0_attn_emb0").reshape(-1), get("L0_attn_emb1").reshape(-1), get("L0_ffn_affinity").T.reshape(-1),
                                get("L0_ffn_router_bias"), get("L0_ffn_te_b2")]).reshape(1, ROW_COLS),
        "wr": rows_to_partitions(get("L0_ffn_Wr").T),
        "te1": rows_to_partitions(get("L0_ffn_te_W1").T),
        "te2": get("L0_ffn_te_W2").T.reshape(2, P, ND).transpose(1, 0, 2),
        "wshared": unit_weights(split_shared(get("L0_ffn_Sg")), split_shared(get("L0_ffn_Su")), get("L0_ffn_Sd").reshape(NS, F, D)),
        "wexperts": unit_weights(get("L0_ffn_Wg"), get("L0_ffn_Wu"), get("L0_ffn_Wd")),
    }
    arrays = {n: np.ascontiguousarray(a) for n, a in arrays.items()}
    nc = bacc.Bacc("TRN2", target_bir_lowering=False, num_devices=1)
    aps = [nc.dram_tensor(n, a.shape, mybir.dt.from_np(a.dtype), kind="ExternalInput").ap() for n, a in arrays.items()]
    aps.append(nc.dram_tensor("out", (N, D), F32, kind="ExternalOutput").ap())
    build(nc, *aps)
    r = run_bass_kernel_spmd(nc, [arrays], core_ids=[0])
    return r.results[0]["out"].reshape(1, N, D)
```
